# Optimizing a Trainium2 kernel written in Bass

```python
import numpy as np
import jax
import jax.numpy as jnp

def _softmax(x, axis=-1):
    return jax.nn.softmax(x, axis=axis)

def _gelu(x):
    return jax.nn.gelu(x, approximate=True)

def _silu(x):
    return jax.nn.silu(x)

def _sigmoid(x):
    return jax.nn.sigmoid(x)

def _layernorm(x, axis=-1, eps=1e-05):
    m = jnp.mean(x, axis=axis, keepdims=True)
    v = jnp.var(x, axis=axis, keepdims=True)
    return (x - m) / jnp.sqrt(v + eps)

def _scatter_add(tgt, idx, src, axis=0):
    return tgt.at[idx].add(src)

def _segment_sum(src, seg, n):
    return jax.ops.segment_sum(src, seg, n)
kernel_name = 'mk_prb_d1_jaxref_r8_70d9e1'

def setup_inputs(seed: int=0):
    np.random.seed(seed)
    _w = jnp.asarray

    def _L0_attn_setup():
        import jax, jax.numpy as jnp
        import numpy as np
        import math
        HID = 256
        HEADS = 16
        HEAD_DIM = HID // HEADS
        SEQ = 512
        BATCH = 1
        ROPE_THETA = 10000.0
        START_RATIO = 0.1
        RECENT_RATIO = 0.25

        def _rope_sin_cos(seq_len, dtype):
            theta = 1.0 / ROPE_THETA ** (jnp.arange(0, HEAD_DIM, 2, dtype=jnp.float32) / HEAD_DIM)
            sinusoid = jnp.arange(seq_len, dtype=jnp.float32)[:, None] * theta[None, :]
            return (jnp.sin(sinusoid).astype(dtype), jnp.cos(sinusoid).astype(dtype))

        def _apply_rope(x, sin, cos):
            x1, x2 = (x[..., 0::2], x[..., 1::2])
            return jnp.concatenate([x1 * cos - x2 * sin, x1 * sin + x2 * cos], axis=-1)
        key = jax.random.key(seed)
        ks = jax.random.split(key, 9)
        s = 0.02
        return {'hidden_states': jax.random.normal(ks[0], (BATCH, SEQ, HID), jnp.float32), 'Wq': jax.random.normal(ks[1], (HID, HID), jnp.float32) * s, 'bq': jnp.zeros((HID,), jnp.float32), 'Wk': jax.random.normal(ks[2], (HID, HID), jnp.float32) * s, 'bk': jnp.zeros((HID,), jnp.float32), 'Wv': jax.random.normal(ks[3], (HID, HID), jnp.float32) * s, 'bv': jnp.zeros((HID,), jnp.float32), 'Wo': jax.random.normal(ks[4], (HID, HID), jnp.float32) * s, 'bo': jnp.zeros((HID,), jnp.float32)}
    _L0_attn_in = _L0_attn_setup()

    def _L0_ffn_setup():
        import jax, jax.numpy as jnp
        import numpy as np
        B, S, H, I, E = (2, 256, 256, 176, 8)
        TOP_K = 2
        key = jax.random.key(seed)
        k0, k1, k2, k3, k4 = jax.random.split(key, 5)
        scale = float(np.sqrt(2.0 / (H + I)))
        return {'hidden_states': jax.random.normal(k0, (B, S, H), dtype=jnp.float32), 'router_w': jax.random.normal(k1, (E, H), dtype=jnp.float32) * H ** (-0.5), 'gate_w': jax.random.normal(k2, (E, I, H), dtype=jnp.float32) * scale, 'up_w': jax.random.normal(k3, (E, I, H), dtype=jnp.float32) * scale, 'down_w': jax.random.normal(k4, (E, H, I), dtype=jnp.float32) * scale}
    _L0_ffn_in = _L0_ffn_setup()
    _d = {'L0_attn_hidden_states': _L0_attn_in['hidden_states'], 'L0_attn_Wq': _L0_attn_in['Wq'], 'L0_attn_bq': _L0_attn_in['bq'], 'L0_attn_Wk': _L0_attn_in['Wk'], 'L0_attn_bk': _L0_attn_in['bk'], 'L0_attn_Wv': _L0_attn_in['Wv'], 'L0_attn_bv': _L0_attn_in['bv'], 'L0_attn_Wo': _L0_attn_in['Wo'], 'L0_attn_bo': _L0_attn_in['bo'], 'L0_ffn_router_w': _L0_ffn_in['router_w'], 'L0_ffn_gate_w': _L0_ffn_in['gate_w'], 'L0_ffn_up_w': _L0_ffn_in['up_w'], 'L0_ffn_down_w': _L0_ffn_in['down_w']}
    _x0 = _d['L0_attn_hidden_states']
    _d['L0_attn_hidden_states'] = jax.random.normal(jax.random.fold_in(jax.random.key(seed), 1), (1, 2048, 256), dtype=_x0.dtype)
    del _x0
    return _d

def reference(L0_attn_hidden_states, L0_attn_Wq, L0_attn_bq, L0_attn_Wk, L0_attn_bk, L0_attn_Wv, L0_attn_bv, L0_attn_Wo, L0_attn_bo, L0_ffn_router_w, L0_ffn_gate_w, L0_ffn_up_w, L0_ffn_down_w):

    def _L0_attn_ref(hidden_states, Wq, bq, Wk, bk, Wv, bv, Wo, bo):
        import jax, jax.numpy as jnp
        import numpy as np
        import math
        HID = 256
        HEADS = 16
        HEAD_DIM = HID // HEADS
        SEQ = 512
        BATCH = 1
        ROPE_THETA = 10000.0
        START_RATIO = 0.1
        RECENT_RATIO = 0.25

        def _rope_sin_cos(seq_len, dtype):
            theta = 1.0 / ROPE_THETA ** (jnp.arange(0, HEAD_DIM, 2, dtype=jnp.float32) / HEAD_DIM)
            sinusoid = jnp.arange(seq_len, dtype=jnp.float32)[:, None] * theta[None, :]
            return (jnp.sin(sinusoid).astype(dtype), jnp.cos(sinusoid).astype(dtype))

        def _apply_rope(x, sin, cos):
            x1, x2 = (x[..., 0::2], x[..., 1::2])
            return jnp.concatenate([x1 * cos - x2 * sin, x1 * sin + x2 * cos], axis=-1)
        b, s, _ = hidden_states.shape

        def proj(W, bias):
            y = jnp.einsum('bsd,ed->bse', hidden_states, W) + bias
            return y.reshape(b, s, HEADS, HEAD_DIM).transpose(0, 2, 1, 3)
        q = proj(Wq, bq)
        k = proj(Wk, bk)
        v = proj(Wv, bv)
        sin, cos = _rope_sin_cos(s, hidden_states.dtype)
        q = _apply_rope(q, sin, cos)
        k = _apply_rope(k, sin, cos)
        scale = 1.0 / math.sqrt(HEAD_DIM)
        scores = jnp.einsum('bhqd,bhkd->bhqk', q, k) * scale
        start_budget = math.ceil(START_RATIO * s)
        recent_budget = math.ceil(RECENT_RATIO * s)
        pos = np.arange(s)
        cam = jnp.asarray((pos < start_budget) | (pos >= s - recent_budget))
        neg = jnp.finfo(scores.dtype).min
        scores = jnp.where(cam[None, None, None, :], scores, neg)
        attn = jax.nn.softmax(scores, axis=-1)
        out = jnp.einsum('bhqk,bhkd->bhqd', attn, v)
        out = out.transpose(0, 2, 1, 3).reshape(b, s, HID)
        return jnp.einsum('bsd,ed->bse', out, Wo) + bo

    def _L0_ffn_ref(hidden_states, router_w, gate_w, up_w, down_w):
        import jax, jax.numpy as jnp
        import numpy as np
        B, S, H, I, E = (2, 256, 256, 176, 8)
        TOP_K = 2
        b, s, h = hidden_states.shape
        e = router_w.shape[0]
        x = hidden_states.reshape(-1, h)
        logits = jnp.einsum('th,eh->te', x, router_w)
        top_vals, top_idx = jax.lax.top_k(logits, TOP_K)
        top_w = jax.nn.softmax(top_vals, axis=-1)
        expert = top_idx[:, 0]
        weight = top_w[:, 0]
        gate = jnp.einsum('th,eih->eti', x, gate_w)
        up = jnp.einsum('th,eih->eti', x, up_w)
        act = jax.nn.silu(gate) * up
        out_e = jnp.einsum('eti,ehi->eth', act, down_w)
        combine = jax.nn.one_hot(expert, e, dtype=x.dtype) * weight[:, None]
        out = jnp.einsum('eth,te->th', out_e, combine)
        return out.reshape(b, s, h)
    x = L0_attn_hidden_states
    xn = _layernorm(x, axis=-1)
    x = x + _L0_attn_ref(xn, L0_attn_Wq, L0_attn_bq, L0_attn_Wk, L0_attn_bk, L0_attn_Wv, L0_attn_bv, L0_attn_Wo, L0_attn_bo) + _L0_ffn_ref(xn, L0_ffn_router_w, L0_ffn_gate_w, L0_ffn_up_w, L0_ffn_down_w)
    return x

_drawn_inputs = setup_inputs


def setup_inputs(seed=0):
    import zlib

    import numpy as np

    out = dict(_drawn_inputs(seed))
    spreads = {'L0_attn_bq': (0.0, 0.8),
     'L0_attn_bk': (0.0, 0.8),
     'L0_attn_bv': (0.0, 0.28),
     'L0_attn_bo': (0.0, 0.1)}
    factors = {'L0_attn_Wq': 8.0, 'L0_attn_Wk': 8.0, 'L0_attn_Wv': 8.0}
    for name, (base, spread) in spreads.items():
        noise = np.random.default_rng([zlib.crc32(name.encode()), seed]).standard_normal(out[name].shape)
        drawn = base * np.exp(spread * noise) if base else spread * noise
        out[name] = jnp.asarray(drawn.astype(out[name].dtype))
    for name, factor in factors.items():
        out[name] = (out[name] * factor).astype(out[name].dtype)
    return out
```

```python
from contextlib import ExitStack

import concourse.bass as bass
from concourse import mybir

ALU = mybir.AluOpType
ACT = mybir.ActivationFunctionType
AX = mybir.AxisListType
F32 = mybir.dt.float32
BF16 = mybir.dt.bfloat16
I32 = mybir.dt.int32
U32 = mybir.dt.uint32

P = 128
S, HID, HEADS = 2048, 256, 16
DH = HID // HEADS
NT = S // P
HC = HID // P
START = -(-S // 10)
RECENT = S // 4
NK = START + RECENT
E, I = 8, 176
IH = I // 2
EPS = 1e-5
SCALE = DH ** -0.5
NSLOT = NT + E - 1
QB = 512
NQB = S // QB
CHUNKS = [(0, P, 0), (P, START - P, 1)] + [
    (START + P * j, P, (S - RECENT) // P + j) for j in range(RECENT // P)]
NCH = len(CHUNKS)
KR = 6 * DH
KM = KR + 2
UNITS = NCH * NQB
RING = 3
VW = 32
LOADS = 12 * 16
ORDER = 2 * ("SMSSMSMP" + "SMSSMSMP" + "SMSSMSP")
assert (ORDER.count("S"), ORDER.count("M"), ORDER.count("P")) == (UNITS, NT, NCH)
ROUNDS = (HEADS - 4) // RING
XR = 4
XB = 6
XROUNDS = (NSLOT - 1 - XB) // XR
XE = XB + XR * XROUNDS
C_ID, C_TRI, C_ONE, C_CNT = 0, P, 2 * P, 3 * P
C_REV = C_CNT + NT
C_SLOT = C_REV + E
C_END = C_SLOT + NSLOT


def layer(nc, x_d, wqk_d, wv_d, wo_d, bqk_d, bvo_d, rt_d, gu_d, dn_d, tab_d, const_d,
          q_dram, k_dram, o_dram, sum_dram, recip_dram, xs_dram, y_dram, out_d):
    with ExitStack() as ctx:
        def sb(name, shape, dt=F32):
            return ctx.enter_context(nc.sbuf_tensor(name, shape, dt))

        def sem(name):
            return ctx.enter_context(nc.semaphore(name))

        x_sb = sb("x_sb", [P, NT, HID])
        xn = sb("xn", [P, NT, HID])
        y_tok = xn
        xnT = sb("xnT", [P, HC, S])
        attnT = xnT
        tab = sb("tab", [P, 2, S])
        wqk = sb("wqk", [P, 4, HC * HID])
        wv = sb("wv", [P, HC * HID])
        wo = sb("wo", [P, HC * HID])
        rt = sb("rt", [P, HC * E])
        bqk = sb("bqk", [P, 4 * HC])
        bvo = sb("bvo", [P, 2 * HID])
        const = sb("const", [P, C_END])
        gu = sb("gu", [P, E * HC * 2 * I])
        dn = sb("dn", [IH, E * 2 * HID])
        probs = sb("probs", [P, RING, S])
        rot = probs[:, :, :].rearrange("p r (a n) -> p r a n", a=4)
        recips = tab
        q_op = [sb(f"q_op{n}", [KM, S], BF16) for n in range(RING)]
        k_op = [sb(f"k_op{n}", [KM, NK], BF16) for n in range(RING)]
        v_all = sb("v_all", [P, HEADS * NCH * VW])
        v_op = [sb(f"v_op{n}", [P, NCH * VW]) for n in range(RING)]
        o_st = [sb(f"o_st{n}", [P, QB]) for n in range(RING)]
        sum_c = sb("sum_c", [P, RING, NT])
        recip_c = sb("recip_c", [P, RING, NT])
        parts = sb("parts", [P, RING, 3, QB], BF16)
        zeros = sb("zeros", [P, HID])
        stats = sb("stats", [P, NT, 6])
        mv = sb("mv", [P, NT, 2])
        var = sb("var", [P, NT])
        std = sb("std", [P, NT])
        rstd = sb("rstd", [P, NT])
        mx = sb("mx", [P, RING, NT])
        neg = sb("neg", [P, RING, 2 * NT], BF16)
        neg_row = sb("neg_row", [2 * NT, RING, P], BF16)
        id16 = sb("id16", [P, P], BF16)
        te = {n: sb("te_" + n, [P, NT, E]) for n in
              ("logit", "best", "rev", "hot", "gone", "rest", "offs", "rank", "row", "mine")}
        tk = {n: sb("tk_" + n, [P, NT]) for n in
              ("top", "pick", "second", "gap", "ratio", "denom", "weight", "row")}
        scan = [sb(f"scan{n}", [P, E, 2 * NT]) for n in range(5)]
        more = sb("more", [P, E, NT])
        tiles = [sb(f"tiles{n}", [P, 2 * E]) for n in range(4)]
        first_row = sb("first_row", [P, E])
        past = sb("past", [P, NSLOT, E - 1])
        expert_f = sb("expert_f", [P, NSLOT])
        expert = sb("expert", [P, NSLOT], I32)
        row_of = sb("row_of", [P, NT], U32)
        ys = [sb(f"ys{n}", [P, HID]) for n in range(XR)]
        temps = probs[:, :, :].rearrange("p r n -> p (r n)")
        xsT, th, ga, hid, hidT = [], [], [], [], []
        at = 0
        for n in range(2):
            for group, rows, size in ((xsT, P, HC * P), (th, P, I), (ga, P, I), (hid, P, I), (hidT, IH, 2 * P)):
                group.append(temps[0:rows, at:at + size])
                at += size
        xs = [o_st[n // 2][:, HID * (n % 2):HID * (n % 2) + HID] for n in range(XR)]
        prob = [probs[:, 0, :], dn[:, 0:S], probs[:, 1, :], probs[:, 2, :],
                wqk[:].rearrange("p w n -> p (w n)"), gu[:, 0:S]]
        ps = ctx.enter_context(nc.psum_tensor("ps", [P, 8 * 512], F32))

        def bank(n):
            return ps[:, 512 * n:512 * n + 512]

        turned_neg = ps[0:2 * NT, 2048 - P // 2:2048].bitcast(BF16)
        ident, tri, ones = (const[:, c:c + P] for c in (C_ID, C_TRI, C_ONE))

        x_in = [sem(f"x_in{g}") for g in range(4)]
        const_in, wqk_in, tab_in = sem("const_in"), sem("wqk_in"), sem("tab_in")
        wv_in, rt_in, expert_w_in, wo_in = (sem(n) for n in ("wv_in", "rt_in", "expert_w_in", "wo_in"))
        dve_step = sem("dve_step")
        var_ready, std_ready, xn_ready = sem("var_ready"), sem("std_ready"), sem("xn_ready")
        xT_in_psum, xnT_ready = sem("xT_in_psum"), sem("xnT_ready")
        logits_ready, logits_read = sem("logits_ready"), sem("logits_read")
        hot_ready, rank_ready, rank_read = sem("hot_ready"), sem("rank_ready"), sem("rank_read")
        gap_ready, ratio_ready, route_ready = sem("gap_ready"), sem("ratio_ready"), sem("route_ready")
        proj_ready, proj_read = sem("proj_ready"), sem("proj_read")
        turned_ready, hi_ready, rest_ready, mid_ready, lo_ready = (
            sem(n) for n in ("turned_ready", "hi_ready", "rest_ready", "mid_ready", "lo_ready"))
        parts_stored = [sem(f"parts_stored{n}") for n in range(RING)]
        v_in_psum, v_read = sem("v_in_psum"), sem("v_read")
        zero_ready, ones_ready, id16_ready = sem("zero_ready"), sem("ones_ready"), sem("id16_ready")
        zero_filled, scattered, residual_ready = (
            sem(n) for n in ("zero_filled", "scattered", "residual_ready"))
        xs_first = sem("xs_first")
        xs_in = [sem(f"xs_in{n}") for n in range(XR)]
        ys_stored = [sem(f"ys_stored{n}") for n in range(XR)]
        xs_turned, xsT_ready, gu_done, tanh_done, half_done, hid_done = (
            sem(n) for n in ("xs_turned", "xsT_ready", "gu_done", "tanh_done", "half_done", "hid_done"))
        hid_turned, hidT_ready, down_done, ys_ready = (
            sem(n) for n in ("hid_turned", "hidT_ready", "down_done", "ys_ready"))
        gathered = sem("gathered")
        qk_loaded, v_loaded = sem("qk_loaded"), sem("v_loaded")
        max_scored, max_reduced = sem("max_scored"), sem("max_reduced")
        neg_hi, neg_ready, neg_turned, neg_copied, neg_loaded = (
            sem(n) for n in ("neg_hi", "neg_ready", "neg_turned", "neg_copied", "neg_loaded"))
        scored, exp_done, pv_done, o_copied, o_stored = (
            sem(n) for n in ("scored", "exp_done", "pv_done", "o_copied", "o_stored"))
        attn_in = [sem(f"attn_in{m}") for m in range(HC)]
        sum_stored, sum_in, recip_done, recip_stored = (
            sem(n) for n in ("sum_stored", "sum_in", "recip_done", "recip_stored"))
        attn_ready, out_proj, y_added, out_ready, out_stored = (
            sem(n) for n in ("attn_ready", "out_proj", "y_added", "out_ready", "out_stored"))

        PROJ = [(0, m, t0, n, c0) for m in range(HC)
                for t0, n, c0 in ((0, START, 0), (S - RECENT, RECENT, START))]
        PROJ += [(1, m, QB * b, QB, QB * b) for m in range(HC) for b in range(NQB)]
        NPROJ = len(PROJ)
        PBANKS = [(0, 1), (2, 3), (5, 6)]
        VBANKS = (4, 7)
        RANK_AT = 2

        block = ctx.enter_context(nc.Block())

        @block.sync
        def _(sp):
            xv = x_d.rearrange("(t p) d -> p t d", p=P)
            for g in range(4):
                sp.dma_start(x_sb[:, 4 * g:4 * g + 4, :], xv[:, 4 * g:4 * g + 4, :]).then_inc(x_in[g], 16)
                if g == 0:
                    sp.dma_start(const[:], const_d).then_inc(const_in, 16)
                    sp.dma_start(rt[:], rt_d).then_inc(rt_in, 16)
            sp.wait_ge(x_in[3], 16)
            sp.dma_start(wqk[:].rearrange("p w n -> p (w n)"), wqk_d).then_inc(wqk_in, 16)
            sp.dma_start(bqk[:], bqk_d).then_inc(wqk_in, 16)
            sp.dma_start(tab[:].rearrange("p a n -> p (a n)"), tab_d).then_inc(tab_in, 16)
            sp.dma_start(wv[:], wv_d).then_inc(wv_in, 16)
            sp.dma_start(bvo[:], bvo_d.broadcast_to([P, 2 * HID])).then_inc(wv_in, 16)
            sp.wait_ge(tab_in, 16)
            sp.dma_start(gu[:], gu_d).then_inc(expert_w_in, 16)
            sp.dma_start(dn[:], dn_d).then_inc(expert_w_in, 16)
            sp.dma_start(wo[:], wo_d).then_inc(wo_in, 16)

            for u, (is_q, m, t0, n, c0) in enumerate(PROJ):
                sp.wait_ge(hi_ready, u + 1)
                sp.wait_ge(mid_ready, u + 1)
                sp.wait_ge(lo_ready, u + 1)
                dst = (q_dram if is_q else k_dram)[:, P * m:P * m + P, c0:c0 + n]
                sp.dma_start(dst.rearrange("s p n -> p s n"),
                             parts[:, u % RING, :, 0:n]).then_inc(parts_stored[u % RING], 16)

            def load_head(h, slot):
                for term, part in enumerate((0, 0, 0, 1, 1, 2)):
                    sp.dma_start(q_op[slot][DH * term:DH * term + DH, :],
                                 q_dram[part, bass.ds(h * DH, DH), :]).then_inc(qk_loaded, 16)
                for term, part in enumerate((0, 1, 2, 0, 1, 0)):
                    sp.dma_start(k_op[slot][DH * term:DH * term + DH, :],
                                 k_dram[part, bass.ds(h * DH, DH), :]).then_inc(qk_loaded, 16)

            def load_xs(t, slot):
                sp.dma_start(xs[slot], xs_dram[bass.ds(t * P, P), :]).then_inc(xs_in[slot], 16)

            def store_ys(t, slot):
                sp.wait_ge(ys_ready, t + 1)
                sp.dma_start(y_dram[bass.ds(t * P, P), :], ys[slot][:]).then_inc(ys_stored[slot], 16)

            def expert_step(t, slot, load=True, store=True):
                if load:
                    sp.wait_ge(xs_turned, t + 1)
                    load_xs(t + XR, slot)
                if store:
                    store_ys(t - 2, (slot - 2) % XR)

            for t in range(XR):
                expert_step(t, t, store=t >= 2)
            for n in range(RING):
                sp.wait_ge(parts_stored[n], 16 * len(range(n, NPROJ, RING)))
            load_head(0, 0)
            with sp.Fori(1, (NSLOT - XR) // XR) as i:
                for j in range(XR):
                    expert_step(i * XR + j, j)
            load_head(1, 1)
            for t in range((NSLOT - XR) // XR * XR, NSLOT + 2):
                expert_step(t, t % XR, load=t + XR < NSLOT)

            def load_neg(h, slot):
                sp.wait_ge(neg_copied, h + 1)
                sp.dma_start(q_op[slot][KR:KM, :].rearrange("s (t p) -> s t p", p=P),
                             neg_row[:, slot, :]).then_inc(neg_loaded, 16)

            def store_o(h, slot):
                sp.wait_ge(o_copied, h + 1)
                sp.dma_start(sum_dram[bass.ds(h, 1), :].rearrange("a (b n) -> (a b) n", b=NQB),
                             o_st[slot][DH:P:VW, :]).then_inc(sum_stored, 16)
                for b in range(NQB):
                    sp.dma_start(o_dram[bass.ds(h * DH, DH), QB * b:QB * b + QB],
                                 o_st[slot][VW * b:VW * b + DH, :]).then_inc(o_stored, 16)
                sp.wait_ge(sum_stored, (h + 1) * 16)
                sp.dma_start(sum_c[:, slot, :], sum_dram[bass.ds(h, 1), :].rearrange("a (p f) -> (a p) f", p=P)
                             ).then_inc(sum_in, 16)

            def store_recip(h, slot):
                sp.wait_ge(recip_done, h + 1)
                sp.dma_start(recip_dram[bass.ds(h, 1), :].rearrange("a (p f) -> (a p) f", p=P),
                             recip_c[:, slot, :]).then_inc(recip_stored, 16)

            def head_step(h, k, first=False, load=True, turn=True):
                if load:
                    if not first:
                        sp.wait_ge(scored, h * UNITS)
                    load_head(h + 2, (k + 2) % RING)
                if not first:
                    store_o(h - 1, (k - 1) % RING)
                if turn:
                    load_neg(h + 1, (k + 1) % RING)
                if not first:
                    store_recip(h - 1, (k - 1) % RING)

            def load_attn(h0, h1, done):
                m, p0, p1 = h0 * DH // P, h0 * DH % P, (h1 - 1) * DH % P + DH
                sp.wait_ge(o_stored, 16 * NQB * h1)
                sp.dma_start(attnT[p0:p1, m, :], o_dram[h0 * DH:h1 * DH, :]).then_inc(done, 16)
                sp.wait_ge(recip_stored, 16 * h1)
                for h in range(h0, h1):
                    sp.dma_start(recips[h * DH % P:h * DH % P + DH, m, :],
                                 recip_dram[h:h + 1, :].broadcast_to([DH, S])).then_inc(done, 16)

            load_neg(0, 0)
            head_step(0, 0, first=True)
            head_step(1, 1)
            with sp.Fori(0, ROUNDS) as i:
                for j in range(RING):
                    head_step(i * RING + 2 + j, (2 + j) % RING)
            head_step(14, 2, load=False)
            load_attn(0, HEADS // 2, attn_in[0])
            head_step(15, 0, load=False, turn=False)
            load_attn(HEADS // 2, HEADS - 1, attn_in[1])
            store_o(15, 0)
            store_recip(15, 0)
            load_attn(HEADS - 1, HEADS, attn_in[1])

            ov = out_d.rearrange("(t p) d -> p t d", p=P)
            for pair in range(NT // 2):
                sp.wait_ge(out_ready, pair + 1)
                sp.dma_start(ov[:, 2 * pair:2 * pair + 2, :], x_sb[:, 2 * pair:2 * pair + 2, :]
                             ).then_inc(out_stored, 16)
            sp.wait_ge(out_stored, 16 * (NT // 2))

        @block.gpsimd
        def _(pool):
            pool.memset(zeros[:], 0.0).then_inc(zero_ready, 1)
            pool.wait_ge(zero_ready, 1)
            pool.wait_ge(tab_in, 16)
            pool.dma_start(xs_dram.rearrange("(t p) d -> p t d", p=P),
                           zeros[:].rearrange("p (a d) -> p a d", a=1).broadcast_to([P, NSLOT, HID])
                           ).then_inc(zero_filled, 16)
            for n in range(RING):
                pool.memset(k_op[n][KR:KM, :], 1.0).then_inc(ones_ready, 1)
                pool.wait_ge(ones_ready, n + 1)
            pool.memset(v_all[:], 1.0).then_inc(ones_ready, 1)

            pool.wait_ge(zero_filled, 16)
            pool.wait_ge(route_ready, 1)
            for t in range(NT):
                pool.indirect_dma_start(
                    out=xs_dram, out_offset=bass.IndirectOffsetOnAxis(ap=row_of[:, t:t + 1], axis=0),
                    in_=xn[:, t, :], in_offset=None).then_inc(scattered, 16)

            pool.wait_ge(scattered, 16 * NT)
            for t in range(XR):
                pool.dma_start(xs[t], xs_dram[P * t:P * t + P, :]).then_inc(xs_first, 16)

            pool.wait_ge(wv_in, 32)
            for t in range(NT):
                ins = pool.tensor_tensor(x_sb[:, t, :], x_sb[:, t, :], bvo[:, HID:2 * HID], ALU.add)
            ins.then_inc(residual_ready, 1)

            def copy_v(h, slot):
                pool.tensor_copy(v_op[slot][:], v_all[:, bass.ds(h * (NCH * VW), NCH * VW)]
                                 ).then_inc(v_loaded, 1)

            pool.wait_ge(v_read, NCH)
            for h in range(RING):
                copy_v(h, h)

            for n in range(XR):
                pool.wait_ge(ys_stored[n], 16 * len(range(n, NSLOT, XR)))
            for t in range(NT):
                pool.indirect_dma_start(
                    out=y_tok[:, t, :], out_offset=None, in_=y_dram,
                    in_offset=bass.IndirectOffsetOnAxis(ap=row_of[:, t:t + 1], axis=0)
                ).then_inc(gathered, 16)

            with pool.Fori(1, 5) as i:
                for k in range(RING):
                    pool.wait_ge(pv_done, (i * RING + (k - 2)) * NCH)
                    copy_v(i * RING + k, k)
            pool.wait_ge(pv_done, (HEADS - 1 - 2) * NCH)
            copy_v(HEADS - 1, 0)

        @block.tensor
        def _(pe):
            pe.wait_ge(const_in, 16)
            for pair in range(NT // 2):
                b = pair % 4
                if pair >= 4:
                    pe.wait_ge(xnT_ready, pair - 3)
                pe.wait_ge(xn_ready, pair // 2 + 1)
                for m in range(HC):
                    for j in range(2):
                        ins = pe.transpose(bank(b)[:, 256 * m + P * j:256 * m + P * j + P],
                                           xn[:, 2 * pair + j, P * m:P * m + P], ident)
                ins.then_inc(xT_in_psum, 1)
            pe.wait_ge(rt_in, 16)
            for t in range(NT):
                pe.wait_ge(xnT_ready, t // 2 + 1)
                for m in range(HC):
                    ins = pe.matmul(bank(4)[:, E * t:E * t + E], xnT[:, m, P * t:P * t + P],
                                    rt[:, E * m:E * m + E], start=m == 0, stop=m == HC - 1)
            ins.then_inc(logits_ready, 1)

            pe.wait_ge(wqk_in, 32)
            for u, (is_q, half, t0, n, c0) in enumerate(PROJ):
                if u == RANK_AT:
                    pe.wait_ge(hot_ready, 1)
                    hot = te["hot"][:].rearrange("p t e -> p (t e)")
                    pe.matmul(bank(7)[:, 0:NT * E], tri, hot, start=True, stop=True)
                    pe.matmul(bank(7)[:, NT * E:2 * NT * E], ones, hot, start=True,
                              stop=True).then_inc(rank_ready, 1)
                if u >= RING:
                    pe.wait_ge(proj_read, 2 * (u - RING + 1))
                for swapped in range(2):
                    w = wqk[:, 2 * is_q + swapped, :]
                    for m in range(HC):
                        ins = pe.matmul(bank(PBANKS[u % RING][swapped])[:, 0:n],
                                        w[:, HID * m + P * half:HID * m + P * half + P],
                                        xnT[:, m, t0:t0 + n], start=m == 0, stop=m == HC - 1)
                ins.then_inc(proj_ready, 1)
            pe.wait_ge(wv_in, 32)
            for c, (c0, rows, tile) in enumerate(CHUNKS):
                if c == 0:
                    pe.wait_ge(logits_read, 1)
                if c == 1:
                    pe.wait_ge(rank_read, 1)
                if c >= 2:
                    pe.wait_ge(v_read, c - 1)
                for m in range(HC):
                    ins = pe.matmul(bank(VBANKS[c % 2])[0:rows, 0:HID], xnT[:, m, P * tile:P * tile + rows],
                                    wv[:, HID * m:HID * m + HID], start=m == 0, stop=m == HC - 1)
                ins.then_inc(v_in_psum, 1)

            def turn_rows(t, b, slot, rnd, static_first=False):
                if isinstance(t, int) and t < XR:
                    pe.wait_ge(xs_first, 16 * XR)
                else:
                    pe.wait_ge(xs_in[slot], rnd * 16)
                if not static_first:
                    pe.wait_ge(xsT_ready, t - 1)
                for m in range(HC):
                    ins = pe.transpose(bank(2 + b)[:, P * m:P * m + P], xs[slot][:, P * m:P * m + P], ident)
                ins.then_inc(xs_turned, 1)

            def gate_up(t, b, free=True):
                e = pe.value_load(expert[0:1, bass.ds(t, 1)], min_val=0, max_val=E - 1)
                pe.wait_ge(xsT_ready, t + 1)
                if free:
                    pe.wait_ge(hid_done, t - 1)
                for m in range(HC):
                    ins = pe.matmul(bank(b)[:, 0:2 * I], xsT[b][:, P * m:P * m + P],
                                    gu[:, bass.ds(e * (HC * 2 * I) + 2 * I * m, 2 * I)],
                                    start=m == 0, stop=m == HC - 1)
                ins.then_inc(gu_done, 1)

            def down(t, b, free=True):
                e = pe.value_load(expert[0:1, bass.ds(t, 1)], min_val=0, max_val=E - 1)
                pe.wait_ge(hidT_ready, t + 1)
                if free:
                    pe.wait_ge(ys_ready, t - 1)
                for m in range(2):
                    ins = pe.matmul(bank(6 + b)[:, 0:HID], hidT[b][:, P * m:P * m + P],
                                    dn[:, bass.ds(e * (2 * HID) + HID * m, HID)],
                                    start=m == 0, stop=m == 1)
                ins.then_inc(down_done, 1)

            def turn_hidden(t, b, free=True):
                pe.wait_ge(hid_done, t + 1)
                if free:
                    pe.wait_ge(hidT_ready, t - 1)
                for m in range(2):
                    ins = pe.transpose(bank(4 + b)[0:IH, P * m:P * m + P], hid[b][:, IH * m:IH * m + IH], ident)
                ins.then_inc(hid_turned, 1)

            def expert_step(s, j, rnd):
                static = isinstance(s, int)
                if not static or s < NSLOT:
                    gate_up(s, j % 2, not static or s >= 2)
                if not static or s + 1 < NSLOT:
                    turn_rows(s + 1, (j + 1) % 2, (j + 1) % XR, rnd, static and s + 1 < 2)
                if not static or s >= 2:
                    down(s - 2, j % 2, not static or s >= 4)
                if not static or 1 <= s <= NSLOT:
                    turn_hidden(s - 1, (j + 1) % 2, not static or s >= 3)

            pe.wait_ge(proj_read, 2 * NPROJ)
            pe.wait_ge(v_read, NCH)
            pe.wait_ge(expert_w_in, 32)
            turn_rows(0, 0, 0, 0, True)
            for s in range(XB):
                expert_step(s, s % XR, (s + 1) // XR)
            with pe.Fori(0, XROUNDS) as i:
                for j in range(XB, XB + XR):
                    expert_step(i * XR + j, j % XR, i + (j + 1) // XR)
            for s in range(XE, NSLOT + 2):
                expert_step(s, s % XR, (s + 1) // XR)

            def max_tile(h, t, slot, head0=False):
                if not head0 or t >= 2:
                    pe.wait_ge(max_reduced, h * NT + t - 1)
                if t == 3 and not head0:
                    pe.wait_ge(neg_copied, h)
                if t == 1 and not head0:
                    turn_neg(h - 1, (slot - 1) % RING)
                at = 1024 * (t % 2)
                for c0, n in ((0, 512), (512, NK - 512)):
                    ins = pe.matmul(ps[:, at + c0:at + c0 + n], q_op[slot][0:KR, P * t:P * t + P],
                                    k_op[slot][0:KR, c0:c0 + n], start=True, stop=True)
                ins.then_inc(max_scored, 1)

            def turn_neg(h, slot):
                pe.wait_ge(neg_ready, h + 1)
                pe.transpose(turned_neg, neg[:, slot, :], id16[:]).then_inc(neg_turned, 1)

            def pv(h, c, slot, head0=False):
                rows = CHUNKS[c][1]
                pe.wait_ge(exp_done, h * UNITS + NQB * (c + 1))
                if c == 0:
                    pe.wait_ge(v_loaded, h + 1)
                    if not head0:
                        pe.wait_ge(o_copied, h)
                for b in range(NQB):
                    ins = pe.matmul(bank(7)[VW * b:VW * b + VW, :], v_op[slot][0:rows, VW * c:VW * c + VW],
                                    prob[c][0:rows, QB * b:QB * b + QB],
                                    start=c == 0, stop=c == NCH - 1)
                ins.then_inc(pv_done, 1)

            def head_step(h, k, first=False, rest_of_next=True, start_after=True):
                u = j = p = 0
                for what in ORDER:
                    if what == "S":
                        c, b = divmod(u, NQB)
                        c0, rows, _ = CHUNKS[c]
                        if not (first and u < RING):
                            pe.wait_ge(exp_done, h * UNITS + u - (RING - 1))
                        if u == 0:
                            pe.wait_ge(neg_loaded, (h + 1) * 16)
                        pe.matmul(bank(4 + u % RING)[0:rows, :], k_op[k][:, c0:c0 + rows],
                                  q_op[k][:, QB * b:QB * b + QB], start=True, stop=True).then_inc(scored, 1)
                        u += 1
                    elif what == "M":
                        if j < NT // 2 and rest_of_next:
                            max_tile(h + 1, NT // 2 + j, (k + 1) % RING)
                        if j >= NT // 2 and start_after:
                            if j == NT // 2:
                                pe.wait_ge(qk_loaded, (h + 3) * LOADS)
                            max_tile(h + 2, j - NT // 2, (k + 2) % RING)
                        if j == NT // 2 + 1 and rest_of_next and not start_after:
                            pe.wait_ge(max_reduced, (h + 2) * NT)
                            turn_neg(h + 1, (k + 1) % RING)
                        j += 1
                    else:
                        if p > 0:
                            pv(h, p - 1, k, first)
                        elif not first:
                            pv(h - 1, NCH - 1, (k - 1) % RING)
                        p += 1

            pe.wait_ge(ones_ready, RING + 1)
            pe.wait_ge(hidT_ready, NSLOT)
            pe.wait_ge(ys_ready, NSLOT)
            pe.wait_ge(qk_loaded, 2 * LOADS)
            for t in range(NT):
                max_tile(0, t, 0, head0=True)
            for t in range(NT // 2):
                max_tile(1, t, 1)
            head_step(0, 0, first=True)
            head_step(1, 1)
            with pe.Fori(0, ROUNDS) as i:
                for j in range(RING):
                    head_step(i * RING + 2 + j, (2 + j) % RING)
            head_step(14, 2, start_after=False)
            head_step(15, 0, rest_of_next=False, start_after=False)
            pv(15, NCH - 1, 0)

            pe.wait_ge(wo_in, 16)
            pe.wait_ge(exp_done, HEADS * UNITS)
            pe.wait_ge(o_copied, HEADS)
            for m in range(HC):
                for t in range(NT):
                    pe.wait_ge(attn_ready, NQB * m + t // 4 + 1)
                    ins = pe.matmul(ps[:, HID * t:HID * t + HID], attnT[:, m, P * t:P * t + P],
                                    wo[:, HID * m:HID * m + HID], start=m == 0 and t % 2 == 0,
                                    stop=m == HC - 1, skip_group_check=True)
                    if m == HC - 1 and t % 2 == 1:
                        ins.then_inc(out_proj, 1)

        @block.vector
        def _(dve):
            steps = [0]

            def step(ins):
                steps[0] += 1
                ins.then_inc(dve_step, 1)

            def settle():
                dve.wait_ge(dve_step, steps[0])

            def moments(g):
                dve.wait_ge(x_in[g], 16)
                for t in range(4 * g, 4 * g + 4):
                    step(dve.bn_stats(stats[:, t, :], x_sb[:, t, :]))
                settle()
                for t in range(4 * g, 4 * g + 4):
                    step(dve.bn_aggr(mv[:, t, :], stats[:, t, :]))
                settle()
                dve.tensor_scalar(var[:, 4 * g:4 * g + 4], mv[:, 4 * g:4 * g + 4, 1], EPS, None,
                                  ALU.add).then_inc(var_ready, 1)

            def normalize(g):
                dve.wait_ge(std_ready, g + 1)
                step(dve.reciprocal(rstd[:, 4 * g:4 * g + 4], std[:, 4 * g:4 * g + 4]))
                settle()
                for t in range(4 * g, 4 * g + 4):
                    ins = dve.tensor_scalar(xn[:, t, :], x_sb[:, t, :], mv[:, t, 0:1], rstd[:, t:t + 1],
                                            ALU.subtract, ALU.mult)
                ins.then_inc(xn_ready, 1)

            moments(0)
            for g in range(1, 4):
                moments(g)
                normalize(g - 1)
            normalize(3)
            dve.wait_ge(const_in, 16)
            dve.tensor_copy(id16[:], ident).then_inc(id16_ready, 1)
            for s_ in scan + tiles:
                step(dve.memset(s_[:], 0.0))

            def over_tokens(ap):
                return ap.rearrange("p (a e) -> p a e", a=1).broadcast_to([P, NT, E])

            def over_experts(ap):
                return ap.rearrange("p (t a) -> p t a", a=1).broadcast_to([P, NT, E])

            rev = over_tokens(const[:, C_REV:C_REV + E])
            dve.wait_ge(logits_ready, 1)
            dve.tensor_copy(te["logit"][:].rearrange("p t e -> p (t e)"),
                            bank(4)[:, 0:NT * E]).then_inc(logits_read, 1)
            dve.wait_ge(logits_read, 1)
            step(dve.tensor_reduce(tk["top"][:], te["logit"][:], AX.X, ALU.max))
            settle()
            step(dve.tensor_tensor(te["best"][:], te["logit"][:], over_experts(tk["top"][:]), ALU.is_equal))
            settle()
            step(dve.tensor_tensor(te["rev"][:], te["best"][:], rev, ALU.mult))
            settle()
            step(dve.tensor_reduce(tk["pick"][:], te["rev"][:], AX.X, ALU.max))
            settle()
            dve.tensor_tensor(te["hot"][:], over_experts(tk["pick"][:]), rev, ALU.is_equal
                              ).then_inc(hot_ready, 1)
            dve.wait_ge(hot_ready, 1)
            step(dve.tensor_scalar(te["gone"][:], te["hot"][:], -3.0e38, None, ALU.mult))
            settle()
            step(dve.tensor_tensor(te["rest"][:], te["logit"][:], te["gone"][:], ALU.add))
            settle()
            step(dve.tensor_reduce(tk["second"][:], te["rest"][:], AX.X, ALU.max))
            settle()
            dve.tensor_tensor(tk["gap"][:], tk["second"][:], tk["top"][:], ALU.subtract
                              ).then_inc(gap_ready, 1)

            def route():
                dve.wait_ge(ratio_ready, 1)
                step(dve.tensor_scalar(tk["denom"][:], tk["ratio"][:], 1.0, None, ALU.add))
                settle()
                step(dve.reciprocal(tk["weight"][:], tk["denom"][:]))
                dve.wait_ge(rank_ready, 1)
                counts = bank(7)[:, NT * E:2 * NT * E].rearrange("p (t e) -> p e t", e=E)
                step(dve.tensor_copy(te["rank"][:].rearrange("p t e -> p (t e)"), bank(7)[:, 0:NT * E]))
                dve.tensor_copy(scan[0][:, :, NT:2 * NT], counts).then_inc(rank_read, 1)
                dve.wait_ge(rank_read, 1)
                settle()
                for n, shift in enumerate((1, 2, 4, 8)):
                    step(dve.tensor_tensor(scan[n + 1][:, :, NT:2 * NT], scan[n][:, :, NT:2 * NT],
                                           scan[n][:, :, NT - shift:2 * NT - shift], ALU.add))
                    settle()
                total = scan[4][:, :, 2 * NT - 1:2 * NT]
                step(dve.tensor_tensor(
                    more[:], total.broadcast_to([P, E, NT]),
                    const[:, C_CNT:C_CNT + NT].rearrange("p (a t) -> p a t", a=1).broadcast_to([P, E, NT]),
                    ALU.is_gt))
                settle()
                step(dve.tensor_reduce(tiles[0][:, E:2 * E], more[:], AX.X, ALU.add))
                settle()
                for n, shift in enumerate((1, 2, 4)):
                    step(dve.tensor_tensor(tiles[n + 1][:, E:2 * E], tiles[n][:, E:2 * E],
                                           tiles[n][:, E - shift:2 * E - shift], ALU.add))
                    settle()
                step(dve.tensor_scalar(first_row[:], tiles[3][:, E - 1:2 * E - 1], float(P), None, ALU.mult))
                step(dve.tensor_tensor(te["offs"][:], scan[4][:, :, NT - 1:2 * NT - 1].rearrange("p e t -> p t e"),
                                       te["rank"][:], ALU.add))
                settle()
                step(dve.tensor_tensor(te["row"][:], te["offs"][:], over_tokens(first_row[:]), ALU.add))
                settle()
                step(dve.tensor_tensor(te["mine"][:], te["row"][:], te["hot"][:], ALU.mult))
                settle()
                step(dve.tensor_reduce(tk["row"][:], te["mine"][:], AX.X, ALU.add))
                ends = tiles[3][:, E:2 * E - 1].rearrange("p (a e) -> p a e", a=1)
                step(dve.tensor_tensor(
                    past[:], ends.broadcast_to([P, NSLOT, E - 1]),
                    const[:, C_SLOT:C_SLOT + NSLOT].rearrange("p (s a) -> p s a", a=1
                                                              ).broadcast_to([P, NSLOT, E - 1]), ALU.is_le))
                settle()
                step(dve.tensor_reduce(expert_f[:], past[:], AX.X, ALU.add))
                settle()
                step(dve.tensor_copy(expert[:], expert_f[:]))
                dve.tensor_copy(row_of[:], tk["row"][:]).then_inc(route_ready, 1)

            def rotate(u):
                is_q, half, t0, n, c0 = PROJ[u]
                r, (a, b) = u % RING, PBANKS[u % RING]
                dve.wait_ge(proj_ready, u + 1)
                if u >= RING:
                    dve.wait_ge(lo_ready, u - RING + 1)
                for swapped, bk in ((0, a), (1, b)):
                    col = HC * (2 * is_q + swapped) + half
                    ins = dve.scalar_tensor_tensor(rot[:, r, swapped, 0:n], bank(bk)[:, 0:n],
                                                   bqk[:, col:col + 1], tab[:, swapped, t0:t0 + n],
                                                   ALU.add, ALU.mult)
                    ins.then_inc(proj_read, 1)
                dve.wait_ge(proj_read, 2 * (u + 1))
                dve.tensor_tensor(rot[:, r, 2, 0:n], rot[:, r, 0, 0:n], rot[:, r, 1, 0:n], ALU.add
                                  ).then_inc(turned_ready, 1)

            def rest(u):
                n, r = PROJ[u][3], u % RING
                dve.wait_ge(turned_ready, u + 1)
                dve.wait_ge(hi_ready, u + 1)
                dve.tensor_tensor(rot[:, r, 3, 0:n], rot[:, r, 2, 0:n], parts[:, r, 0, 0:n], ALU.subtract
                                  ).then_inc(rest_ready, 1)

            def lowest(u):
                n, r = PROJ[u][3], u % RING
                dve.wait_ge(mid_ready, u + 1)
                dve.tensor_tensor(parts[:, r, 2, 0:n], rot[:, r, 3, 0:n], parts[:, r, 1, 0:n], ALU.subtract
                                  ).then_inc(lo_ready, 1)

            dve.wait_ge(wqk_in, 32)
            dve.wait_ge(tab_in, 16)
            for u in range(NPROJ + 2):
                if u == RANK_AT - 1:
                    route()
                if u < NPROJ:
                    rotate(u)
                if 1 <= u <= NPROJ:
                    rest(u - 1)
                if u >= 2:
                    lowest(u - 2)

            dve.wait_ge(ones_ready, RING + 1)
            dve.wait_ge(wv_in, 32)
            v_view = v_all[:].rearrange("p (h c w) -> p h c w", h=HEADS, c=NCH)
            for c, (c0, rows, tile) in enumerate(CHUNKS):
                dve.wait_ge(v_in_psum, c + 1)
                dve.tensor_tensor(v_view[0:rows, :, c, 0:DH],
                                  bank(VBANKS[c % 2])[0:rows, 0:HID].rearrange("p (h d) -> p h d", h=HEADS),
                                  bvo[0:rows, 0:HID].rearrange("p (h d) -> p h d", h=HEADS),
                                  ALU.add).then_inc(v_read, 1)

            def expert_step(s, b):
                static = isinstance(s, int)
                if not static or s < NSLOT:
                    dve.wait_ge(tanh_done, s + 1)
                    if not static or s >= 2:
                        dve.wait_ge(hid_done, s - 1)
                    dve.scalar_tensor_tensor(ga[b], th[b], 1.0, bank(b)[:, 0:I], ALU.add, ALU.mult
                                             ).then_inc(half_done, 1)
                    dve.wait_ge(half_done, s + 1)
                    if not static or s >= 2:
                        dve.wait_ge(hid_turned, s - 1)
                    dve.scalar_tensor_tensor(hid[b], ga[b], 0.5, bank(b)[:, I:2 * I], ALU.mult, ALU.mult
                                             ).then_inc(hid_done, 1)
                if not static or 1 <= s <= NSLOT:
                    dve.wait_ge(hid_turned, s)
                    if not static or s >= 3:
                        dve.wait_ge(down_done, s - 2)
                    dve.tensor_copy(hidT[1 - b], bank(4 + 1 - b)[0:IH, 0:2 * P]).then_inc(hidT_ready, 1)

            for s in range(XB):
                expert_step(s, s % 2)
            with dve.Fori(0, XROUNDS) as i:
                for j in range(XB, XB + XR):
                    expert_step(i * XR + j, j % 2)
            for s in range(XE, NSLOT + 1):
                expert_step(s, s % 2)

            def reduce_tile(h, t, slot):
                dve.wait_ge(max_scored, h * NT + t + 1)
                at = 1024 * (t % 2)
                dve.tensor_reduce(mx[:, slot, t:t + 1], ps[:, at:at + NK], AX.X, ALU.max
                                  ).then_inc(max_reduced, 1)

            def negate(h, slot):
                dve.wait_ge(max_reduced, (h + 1) * NT)
                dve.tensor_scalar(neg[:, slot, 0:NT], mx[:, slot, :], -1.0, None, ALU.mult
                                  ).then_inc(neg_hi, 1)
                dve.wait_ge(neg_hi, h + 1)
                dve.scalar_tensor_tensor(neg[:, slot, NT:2 * NT], mx[:, slot, :], -1.0,
                                         neg[:, slot, 0:NT], ALU.mult, ALU.subtract
                                         ).then_inc(neg_ready, 1)

            def copy_neg(h, slot, early=False):
                dve.wait_ge(neg_turned, h + 1)
                if not early:
                    dve.wait_ge(neg_loaded, (h - 2) * 16)
                dve.tensor_copy(neg_row[:, slot, :], turned_neg).then_inc(neg_copied, 1)

            def invert(h, slot):
                dve.wait_ge(sum_in, (h + 1) * 16)
                if not (isinstance(h, int) and h == 0):
                    dve.wait_ge(recip_stored, h * 16)
                dve.reciprocal(recip_c[:, slot, :], sum_c[:, slot, :]).then_inc(recip_done, 1)

            def head_step(h, k, rest_of_next=True, start_after=True, early=False):
                if rest_of_next:
                    for t in range(NT // 2, NT):
                        reduce_tile(h + 1, t, (k + 1) % RING)
                    negate(h + 1, (k + 1) % RING)
                if start_after:
                    for t in range(2):
                        reduce_tile(h + 2, t, (k + 2) % RING)
                if rest_of_next:
                    copy_neg(h + 1, (k + 1) % RING, early)
                if start_after:
                    for t in range(2, NT // 2):
                        reduce_tile(h + 2, t, (k + 2) % RING)
                if not (isinstance(h, int) and h == 0):
                    invert(h - 1, (k - 1) % RING)

            for t in range(NT):
                reduce_tile(0, t, 0)
            negate(0, 0)
            for t in range(NT // 2):
                reduce_tile(1, t, 1)
                if t == 1:
                    copy_neg(0, 0, early=True)
            head_step(0, 0, early=True)
            head_step(1, 1, early=True)
            with dve.Fori(0, ROUNDS) as i:
                for j in range(RING):
                    head_step(i * RING + 2 + j, (2 + j) % RING)
            head_step(14, 2, start_after=False)

            dve.wait_ge(residual_ready, 1)
            dve.wait_ge(gathered, 16 * NT)
            for t in range(NT):
                dve.scalar_tensor_tensor(x_sb[:, t, :], y_tok[:, t, :], tk["weight"][:, t:t + 1],
                                         x_sb[:, t, :], ALU.mult, ALU.add).then_inc(y_added, 1)
            invert(14, 2)
            def divide(m):
                for b in range(NQB):
                    cols = slice(QB * b, QB * b + QB)
                    dve.tensor_tensor(attnT[:, m, cols], attnT[:, m, cols], recips[:, m, cols], ALU.mult
                                      ).then_inc(attn_ready, 1)

            dve.wait_ge(attn_in[0], 16 * (1 + HEADS // 2))
            divide(0)
            invert(15, 0)
            dve.wait_ge(attn_in[1], 16 * (2 + HEADS // 2))
            divide(1)
            dve.wait_ge(y_added, NT)
            for pair in range(NT // 2):
                dve.wait_ge(out_proj, pair + 1)
                both = x_sb[:, 2 * pair:2 * pair + 2, :].rearrange("p t d -> p (t d)")
                dve.tensor_tensor(both, bank(pair), both, ALU.add).then_inc(out_ready, 1)

        @block.scalar
        def _(act):
            def root(g):
                act.wait_ge(var_ready, g + 1)
                act.activation(std[:, 4 * g:4 * g + 4], var[:, 4 * g:4 * g + 4], ACT.Sqrt
                               ).then_inc(std_ready, 1)

            def copy_xT(pair):
                act.wait_ge(xT_in_psum, pair + 1)
                act.copy(xnT[:, :, 2 * P * pair:2 * P * pair + 2 * P],
                         bank(pair % 4).rearrange("p (m n) -> p m n", m=HC)).then_inc(xnT_ready, 1)

            root(0)
            for g in range(1, 4):
                root(g)
                copy_xT(2 * g - 2)
                copy_xT(2 * g - 1)
            copy_xT(6)
            copy_xT(7)
            act.wait_ge(gap_ready, 1)
            act.activation(tk["ratio"][:], tk["gap"][:], ACT.Exp).then_inc(ratio_ready, 1)

            def highest(u):
                n, r = PROJ[u][3], u % RING
                act.wait_ge(turned_ready, u + 1)
                if u >= RING:
                    act.wait_ge(parts_stored[r], 16 * (u // RING))
                act.copy(parts[:, r, 0, 0:n], rot[:, r, 2, 0:n]).then_inc(hi_ready, 1)

            def middle(u):
                n, r = PROJ[u][3], u % RING
                act.wait_ge(rest_ready, u + 1)
                act.copy(parts[:, r, 1, 0:n], rot[:, r, 3, 0:n]).then_inc(mid_ready, 1)

            for u in range(NPROJ + 1):
                if u < NPROJ:
                    highest(u)
                if u >= 1:
                    middle(u - 1)

            def copy_rows(t, b, static_first=False):
                act.wait_ge(xs_turned, t + 1)
                if not static_first:
                    act.wait_ge(gu_done, t - 1)
                act.copy(xsT[b], bank(2 + b)[:, 0:HC * P]).then_inc(xsT_ready, 1)

            def expert_step(s, j, rnd):
                static = isinstance(s, int)
                b = j % 2
                if not static or s < NSLOT:
                    act.wait_ge(gu_done, s + 1)
                    if not static or s >= 2:
                        act.wait_ge(half_done, s - 1)
                    act.activation(th[b], bank(b)[:, 0:I], ACT.Tanh, scale=0.5).then_inc(tanh_done, 1)
                if not static or s + 1 < NSLOT:
                    copy_rows(s + 1, 1 - b, static and s + 1 < 2)
                if not static or s >= 2:
                    slot = (j - 2) % XR
                    act.wait_ge(down_done, s - 1)
                    if not static or rnd > 0:
                        act.wait_ge(ys_stored[slot], rnd * 16)
                    act.copy(ys[slot][:], bank(6 + b)[:, 0:HID]).then_inc(ys_ready, 1)

            copy_rows(0, 0, True)
            for s in range(XB):
                expert_step(s, s % XR, (s - 2) // XR)
            with act.Fori(0, XROUNDS) as i:
                for j in range(XB, XB + XR):
                    expert_step(i * XR + j, j % XR, i + (j - 2) // XR)
            for s in range(XE, NSLOT + 2):
                expert_step(s, s % XR, (s - 2) // XR)

            def copy_o(h, slot):
                act.wait_ge(pv_done, (h + 1) * NCH)
                if not (isinstance(h, int) and h == 0):
                    act.wait_ge(o_stored, h * (16 * NQB))
                act.copy(o_st[slot][:], bank(7)).then_inc(o_copied, 1)

            def head_step(h, k, first=False):
                for u in range(UNITS):
                    c, b = divmod(u, NQB)
                    rows = CHUNKS[c][1]
                    if b == 0 and not first:
                        act.wait_ge(pv_done, h * NCH + (c + 1 - NCH))
                    act.wait_ge(scored, h * UNITS + u + 1)
                    act.activation(prob[c][0:rows, QB * b:QB * b + QB], bank(4 + u % RING)[0:rows, :],
                                   ACT.Exp, scale=SCALE).then_inc(exp_done, 1)
                    if u == NQB and not first:
                        copy_o(h - 1, (k - 1) % RING)

            head_step(0, 0, first=True)
            head_step(1, 1)
            with act.Fori(0, ROUNDS) as i:
                for j in range(RING):
                    head_step(i * RING + 2 + j, (2 + j) % RING)
            for h in (14, 15):
                head_step(h, h % RING)
            copy_o(HEADS - 1, 0)


def _tables():
    import numpy as np
    f = np.float32
    theta = f(1.0) / np.power(f(10000.0), np.arange(0, DH, 2, dtype=f) / f(DH))
    angle = np.arange(S, dtype=f)[:, None] * theta[None, :]
    sin, cos = np.sin(angle).T, np.cos(angle).T
    cos2 = np.repeat(cos, 2, axis=0)
    sin2 = np.stack([-sin, sin], axis=1).reshape(DH, S)
    tab = np.stack([np.tile(cos2, (P // DH, 1)), np.tile(sin2, (P // DH, 1))], axis=1)
    const = np.zeros((P, C_END), f)
    const[:, C_ID:C_ID + P] = np.eye(P)
    const[:, C_TRI:C_TRI + P] = np.triu(np.ones((P, P)), 1)
    const[:, C_ONE:C_ONE + P] = 1.0
    const[:, C_CNT:C_CNT + NT] = P * np.arange(NT)
    const[:, C_REV:C_REV + E] = E - np.arange(E)
    const[:, C_SLOT:C_SLOT + NSLOT] = np.arange(NSLOT)
    return np.ascontiguousarray(tab.reshape(P, 2 * S), f), const


def kernel(L0_attn_hidden_states, L0_attn_Wq, L0_attn_bq, L0_attn_Wk, L0_attn_bk, L0_attn_Wv, L0_attn_bv,
           L0_attn_Wo, L0_attn_bo, L0_ffn_router_w, L0_ffn_gate_w, L0_ffn_up_w, L0_ffn_down_w):
    import numpy as np
    import concourse.bacc as bacc
    from concourse.bass_utils import run_bass_kernel_spmd

    swap = np.arange(HID).reshape(-1, 2)[:, ::-1].reshape(-1)

    def turned(w):
        w = np.asarray(w)
        return w.T.reshape(HC, P, -1).transpose(1, 0, 2).reshape(P, -1)

    def column(b):
        return np.asarray(b).reshape(HC, P).T

    wk, wq, bk, bq = (np.asarray(a) for a in (L0_attn_Wk, L0_attn_Wq, L0_attn_bk, L0_attn_bq))
    gate_up = np.concatenate([np.asarray(L0_ffn_gate_w), np.asarray(L0_ffn_up_w)], axis=1)
    gate_up = gate_up.transpose(0, 2, 1).reshape(E, HC, P, 2 * I).transpose(2, 0, 1, 3).reshape(P, -1)
    down = np.asarray(L0_ffn_down_w).transpose(0, 2, 1).reshape(E, 2, IH, HID).transpose(2, 0, 1, 3)
    tab, const = _tables()
    arrays = {
        "x": np.asarray(L0_attn_hidden_states).reshape(S, HID),
        "wqk": np.concatenate([turned(wk), turned(wk[swap]), turned(wq), turned(wq[swap])], axis=1),
        "wv": turned(L0_attn_Wv),
        "wo": turned(L0_attn_Wo),
        "bqk": np.concatenate([column(bk), column(bk[swap]), column(bq), column(bq[swap])], axis=1),
        "bvo": np.concatenate([np.asarray(L0_attn_bv), np.asarray(L0_attn_bo)]).reshape(1, 2 * HID),
        "rt": turned(L0_ffn_router_w),
        "gu": gate_up,
        "dn": down.reshape(IH, -1),
        "tab": tab,
        "const": const,
    }
    arrays = {n + "_in": np.ascontiguousarray(a) for n, a in arrays.items()}
    nc = bacc.Bacc("TRN2", target_bir_lowering=False, num_devices=1)
    ins = [nc.dram_tensor(n, a.shape, F32, kind="ExternalInput").ap() for n, a in arrays.items()]
    scratch = [nc.dram_tensor(n, shape, dt, kind="Internal").ap() for n, shape, dt in (
        ("q_parts", (3, HID, S), BF16), ("k_parts", (3, HID, NK), BF16),
        ("attn_out", (HID, S), F32), ("softmax_sums", (HEADS, S), F32),
        ("softmax_recips", (HEADS, S), F32), ("sorted_rows", (NSLOT * P, HID), F32),
        ("sorted_results", (NSLOT * P, HID), F32))]
    out = nc.dram_tensor("out", (S, HID), F32, kind="ExternalOutput").ap()
    layer(nc, *ins, *scratch, out)
    res = run_bass_kernel_spmd(nc, [arrays], core_ids=[0])
    return res.results[0]["out"].reshape(1, S, HID)
```

```python
from contextlib import ExitStack

import concourse.bass as bass
from concourse import mybir

ALU = mybir.AluOpType
ACT = mybir.ActivationFunctionType
AX = mybir.AxisListType
F32 = mybir.dt.float32
BF16 = mybir.dt.bfloat16
I32 = mybir.dt.int32
U32 = mybir.dt.uint32

P = 128
S, HID, HEADS = 2048, 256, 16
DH = HID // HEADS
NT = S // P
HC = HID // P
START = -(-S // 10)
RECENT = S // 4
NK = START + RECENT
E, I = 8, 176
IH = I // 2
EPS = 1e-5
SCALE = DH ** -0.5
NSLOT = NT + E - 1
QB = 512
NQB = S // QB
CHUNKS = [(0, P, 0), (P, START - P, 1)] + [
    (START + P * j, P, (S - RECENT) // P + j) for j in range(RECENT // P)]
NCH = len(CHUNKS)
KR = 6 * DH
KM = KR + 2
UNITS = NCH * NQB
RING = 3
VW = 32
LOADS = 12 * 16
ORDER = 2 * ("MSSMSSMP" + "MSSMSSMP" + "MSSMSSP")
assert (ORDER.count("S"), ORDER.count("M"), ORDER.count("P")) == (UNITS, NT, NCH)
ROUNDS = (HEADS - 4) // RING
XR = 4
XB = 6
XROUNDS = (NSLOT - 1 - XB) // XR
XE = XB + XR * XROUNDS
assert XE - XB == NT
EARLY_MAX = 6 * 512
FIRST_AT = {0: EARLY_MAX, 1: 0, 2: 1024, 3: EARLY_MAX}
C_ID, C_TRI, C_ONE, C_CNT = 0, P, 2 * P, 3 * P
C_REV = C_CNT + NT
C_SLOT = C_REV + E
C_END = C_SLOT + NSLOT


def layer(nc, x_d, wqk_d, wv_d, wo_d, bqk_d, bvo_d, rt_d, gu_d, dn_d, tab_d, const_d,
          q_dram, k_dram, o_dram, sum_dram, recip_dram, xs_dram, y_dram, out_d):
    with ExitStack() as ctx:
        def sb(name, shape, dt=F32):
            return ctx.enter_context(nc.sbuf_tensor(name, shape, dt))

        def sem(name):
            return ctx.enter_context(nc.semaphore(name))

        x_sb = sb("x_sb", [P, NT, HID])
        xn = sb("xn", [P, NT, HID])
        y_tok = xn
        xnT = sb("xnT", [P, HC, S])
        attnT = xnT
        tab = sb("tab", [P, 2, S])
        wqk = sb("wqk", [P, 4, HC * HID])
        wv = sb("wv", [P, HC * HID])
        wo = sb("wo", [P, HC * HID])
        rt = sb("rt", [P, HC * VW])
        bqk = sb("bqk", [P, 2 * HC])
        bvo = sb("bvo", [P, 2 * HID])
        const = sb("const", [P, C_END])
        gu = sb("gu", [P, E * HC * 2 * I])
        dn = sb("dn", [IH, E * 2 * HID])
        probs = sb("probs", [P, RING, S])
        rot = probs[:, :, :].rearrange("p r (a n) -> p r a n", a=4)
        recips = tab
        q_op = [sb(f"q_op{n}", [KM, S], BF16) for n in range(RING)]
        k_op = [sb(f"k_op{n}", [KM, NK], BF16) for n in range(RING)]
        v_all = sb("v_all", [P, HEADS * NCH * VW])
        v_op = [sb(f"v_op{n}", [P, NCH * VW]) for n in range(RING)]
        o_st = [sb(f"o_st{n}", [P, QB]) for n in range(RING)]
        sum_c = sb("sum_c", [P, RING, NT])
        recip_c = sb("recip_c", [P, RING, NT])
        parts = sb("parts", [P, 2, 3, 2, QB], BF16)
        zeros = sb("zeros", [P, HID])
        stats = sb("stats", [P, NT, 6])
        mv = sb("mv", [P, NT, 2])
        var = sb("var", [P, NT])
        std = sb("std", [P, NT])
        rstd = sb("rstd", [P, NT])
        shift = sb("shift", [P, NT])
        mx = sb("mx", [P, RING, NT])
        neg = sb("neg", [P, RING, 2 * NT], BF16)
        neg_row = sb("neg_row", [2 * NT, RING, P], BF16)
        id16 = sb("id16", [P, P], BF16)
        te = {n: sb("te_" + n, [P, NT, E]) for n in
              ("logit", "best", "rev", "hot", "gone", "rest", "offs", "rank", "row", "mine")}
        tk = {n: sb("tk_" + n, [P, NT]) for n in
              ("top", "pick", "second", "gap", "ratio", "denom", "weight", "row")}
        scan = [o_st[1 + n // 2][:, QB // 2 * (n % 2):QB // 2 * (n % 2) + QB // 2].rearrange(
            "p (e t) -> p e t", e=E) for n in range(4)] + [sb("scan4", [P, E, 2 * NT])]
        more = sb("more", [P, E, NT])
        tiles = [sb(f"tiles{n}", [P, 2 * E]) for n in range(4)]
        first_row = sb("first_row", [P, E])
        past = sb("past", [P, NSLOT, E - 1])
        expert_f = sb("expert_f", [P, NSLOT])
        expert = sb("expert", [P, NSLOT], I32)
        row_of = sb("row_of", [P, NT], U32)
        ys = [sb(f"ys{n}", [P, HID]) for n in range(XR)]
        temps = probs[:, :, :].rearrange("p r n -> p (r n)")
        xsT, th, ga, hid, hidT = [], [], [], [], []
        at = 0
        for n in range(2):
            for group, rows, size in ((xsT, P, HC * P), (th, P, I), (ga, P, I), (hid, P, I)):
                group.append(temps[0:rows, at:at + size])
                at += size
            hidT.append((temps[:, at:at + 2 * P] if n == 0 else zeros)[0:IH, :])
            at += 2 * P if n == 0 else 0
        logits_T = o_st[0]
        xs = [o_st[n // 2][:, HID * (n % 2):HID * (n % 2) + HID] for n in range(XR)]
        last_recip = o_st[1]
        prob = [probs[:, 0, :], dn[:, 0:S], probs[:, 1, :], probs[:, 2, :],
                wqk[:].rearrange("p w n -> p (w n)"), gu[:, 0:S]]
        ps = ctx.enter_context(nc.psum_tensor("ps", [P, 8 * 512], F32))

        def bank(n):
            return ps[:, 512 * n:512 * n + 512]

        turned_neg = ps[0:2 * NT, 2048 - P // 2:2048].bitcast(BF16)
        early_turned_neg = ps[0:2 * NT, 4096 - P // 2:4096].bitcast(BF16)
        ident, tri, ones = (const[:, c:c + P] for c in (C_ID, C_TRI, C_ONE))

        x_in = [sem(f"x_in{g}") for g in range(4)]
        x_first = sem("x_first")
        const_in, wqk_in, tab_in = sem("const_in"), sem("wqk_in"), sem("tab_in")
        wv_in, rt_in, expert_w_in, wo_in = (sem(n) for n in ("wv_in", "rt_in", "expert_w_in", "wo_in"))
        dve_step = sem("dve_step")
        var_ready, std_ready, xn_ready = sem("var_ready"), sem("std_ready"), sem("xn_ready")
        scale_ready, xn_on_act = sem("scale_ready"), sem("xn_on_act")
        last_xnT_ready = sem("last_xnT_ready")
        xT_in_psum, xnT_ready = sem("xT_in_psum"), sem("xnT_ready")
        logits_ready, logits_read = sem("logits_ready"), sem("logits_read")
        logits_T_ready, logits_T_copied = sem("logits_T_ready"), sem("logits_T_copied")
        hot_ready, rank_ready, rank_read = sem("hot_ready"), sem("rank_ready"), sem("rank_read")
        gap_ready, ratio_ready, route_ready = sem("gap_ready"), sem("ratio_ready"), sem("route_ready")
        proj_ready, proj_read = sem("proj_ready"), sem("proj_read")
        turned_ready, hi_ready, rest_ready, mid_ready, lo_ready = (
            sem(n) for n in ("turned_ready", "hi_ready", "rest_ready", "mid_ready", "lo_ready"))
        lo_on_pool = sem("lo_on_pool")
        parts_stored = [sem(f"parts_stored{n}") for n in range(2)]
        v_in_psum, v_read = sem("v_in_psum"), sem("v_read")
        zero_ready, ones_ready, id16_ready = sem("zero_ready"), sem("ones_ready"), sem("id16_ready")
        zero_filled, scattered, residual_ready = (
            sem(n) for n in ("zero_filled", "scattered", "residual_ready"))
        xs_first = sem("xs_first")
        xs_in = [sem(f"xs_in{n}") for n in range(XR)]
        ys_stored = [sem(f"ys_stored{n}") for n in range(XR)]
        xs_turned, xsT_ready, gu_done, tanh_done, half_done, hid_done = (
            sem(n) for n in ("xs_turned", "xsT_ready", "gu_done", "tanh_done", "half_done", "hid_done"))
        hid_turned, hidT_ready, down_done, ys_ready = (
            sem(n) for n in ("hid_turned", "hidT_ready", "down_done", "ys_ready"))
        gathered = sem("gathered")
        qk_loaded, v_loaded = sem("qk_loaded"), sem("v_loaded")
        late_q_loaded = sem("late_q_loaded")
        max_scored, max_reduced = sem("max_scored"), sem("max_reduced")
        neg_hi, neg_ready, neg_turned, neg_copied, neg_loaded = (
            sem(n) for n in ("neg_hi", "neg_ready", "neg_turned", "neg_copied", "neg_loaded"))
        scored, exp_done, pv_done, o_copied, o_stored = (
            sem(n) for n in ("scored", "exp_done", "pv_done", "o_copied", "o_stored"))
        attn_in = [sem(f"attn_in{n}") for n in range(3)]
        last_in = [sem(f"last_in{b}") for b in range(NQB)]
        last_inverted = sem("last_inverted")
        sum_stored, sum_in, recip_done, recip_stored = (
            sem(n) for n in ("sum_stored", "sum_in", "recip_done", "recip_stored"))
        attn_ready, out_proj, y_added, out_ready, out_stored = (
            sem(n) for n in ("attn_ready", "out_proj", "y_added", "out_ready", "out_stored"))

        PROJ = [(0, 0, START, 0), (0, S - RECENT, RECENT, START)] + [
            (1, QB * b, QB, QB * b) for b in range(NQB)]
        NPROJ = len(PROJ)
        LAST = NPROJ - 1
        PBANKS = [(0, 1), (2, 3), (5, 6), (0, 1), (2, 3), (6, 7)]
        VBANKS = (4, 7, 4, 7, 4, 5)
        LOW_ON_POOL = (3, 4, 5)
        V_AFTER = {1: (0, 1), 3: (2, 3), 4: (4, 5)}
        V_READ_AT = {2: (0, 1), 3: (2, 3), 4: (4, 5)}
        RANK_AT = 1

        def wait_lowest(engine, u):
            if u in LOW_ON_POOL:
                engine.wait_ge(lo_on_pool, LOW_ON_POOL.index(u) + 1)
            else:
                engine.wait_ge(lo_ready, u + 1 - len([n for n in LOW_ON_POOL if n < u]))

        def form_lowest(engine, u):
            n, r = PROJ[u][2], u % RING
            engine.wait_ge(mid_ready, u + 1)
            engine.tensor_tensor(parts[:, u % 2, 2, :, 0:n], rot[:, r, 1:4:2, 0:n], parts[:, u % 2, 1, :, 0:n],
                                 ALU.subtract).then_inc(lo_on_pool if u in LOW_ON_POOL else lo_ready, 1)

        block = ctx.enter_context(nc.Block())

        @block.sync
        def _(sp):
            xv = x_d.rearrange("(t p) d -> p t d", p=P)
            sp.dma_start(x_sb[:, 0:2, :], xv[:, 0:2, :]).then_inc(x_first, 16)
            for g in range(4):
                t0 = 4 * g if g else 2
                sp.dma_start(x_sb[:, t0:4 * g + 4, :], xv[:, t0:4 * g + 4, :]).then_inc(x_in[g], 16)
                if g == 1:
                    sp.dma_start(const[:], const_d).then_inc(const_in, 16)
                    sp.dma_start(rt[:], rt_d).then_inc(rt_in, 16)
            sp.dma_start(wqk[:, 0:2, :].rearrange("p w n -> p (w n)"), wqk_d).then_inc(wqk_in, 16)
            sp.dma_start(bqk[:], bqk_d).then_inc(wqk_in, 16)
            sp.dma_start(tab[:].rearrange("p a n -> p (a n)"), tab_d).then_inc(tab_in, 16)
            sp.dma_start(wv[:], wv_d).then_inc(wv_in, 16)
            sp.dma_start(bvo[:], bvo_d.broadcast_to([P, 2 * HID])).then_inc(wv_in, 16)
            def store_part(u, part):
                is_q, t0, n, c0 = PROJ[u]
                if part < 2:
                    sp.wait_ge((hi_ready, mid_ready)[part], u + 1)
                else:
                    wait_lowest(sp, u)
                dst = (q_dram if is_q else k_dram)[part, :, c0:c0 + n].rearrange("(p two) n -> p two n", two=2)
                sp.dma_start(dst, parts[:, u % 2, part, :, 0:n]).then_inc(parts_stored[u % 2], 16)

            sp.wait_ge(ones_ready, 1)
            sp.dma_start(gu[:], gu_d).then_inc(expert_w_in, 16)
            sp.dma_start(dn[:], dn_d).then_inc(expert_w_in, 16)
            sp.dma_start(wo[:], wo_d).then_inc(wo_in, 16)

            def load_q(h, slot, term, c0=0, c1=S, done=qk_loaded):
                part = (0, 0, 0, 1, 1, 2)[term]
                sp.dma_start(q_op[slot][DH * term:DH * term + DH, c0:c1],
                             q_dram[part, bass.ds(h * DH, DH), c0:c1]).then_inc(done, 16)

            def load_k(h, slot, term):
                part = (0, 1, 2, 0, 1, 0)[term]
                sp.dma_start(k_op[slot][DH * term:DH * term + DH, :],
                             k_dram[part, bass.ds(h * DH, DH), :]).then_inc(qk_loaded, 16)

            def load_head(h, slot):
                for term in range(6):
                    load_q(h, slot, term)
                    load_k(h, slot, term)

            def load_xs(t, slot):
                sp.dma_start(xs[slot], xs_dram[bass.ds(t * P, P), :]).then_inc(xs_in[slot], 16)

            def store_ys(t, slot):
                sp.wait_ge(ys_ready, t + 1)
                sp.dma_start(y_dram[bass.ds(t * P, P), :], ys[slot][:]).then_inc(ys_stored[slot], 16)

            def expert_step(t, slot, load=True, store=True):
                if load:
                    sp.wait_ge(xs_turned, t + 1)
                    load_xs(t + XR, slot)
                if store:
                    store_ys(t - 2, (slot - 2) % XR)

            for u in range(3):
                for part in range(3):
                    store_part(u, part)
            for n in range(2):
                sp.wait_ge(parts_stored[n], 48)
            for term in range(6):
                load_k(0, 0, term)
            for part in range(3):
                store_part(3, part)
            expert_step(0, 0, store=False)
            for n in range(2):
                sp.wait_ge(parts_stored[n], 2 * 48)
            for term in range(6):
                load_q(0, 0, term, 0, S // 2)
            for part in range(3):
                store_part(4, part)
            for t in range(1, 3 * XR):
                expert_step(t, t % XR, store=t >= 2)
                if t == 5:
                    store_part(LAST, 0)
                    store_part(LAST, 1)
                if t == 6:
                    store_part(LAST, 2)
                if t == 8:
                    for n in range(2):
                        sp.wait_ge(parts_stored[n], 3 * 48)
                    for term in range(6):
                        load_q(0, 0, term, S // 2, S, late_q_loaded)
                if t >= 9:
                    for term in (2 * (t - 9), 2 * (t - 9) + 1):
                        load_q(1, 1, term)
                        load_k(1, 1, term)
            with sp.Fori(3, (NSLOT - XR) // XR) as i:
                for j in range(XR):
                    expert_step(i * XR + j, j)
            tail = range((NSLOT - XR) // XR * XR, NSLOT + 2)
            for t in tail[:-2]:
                expert_step(t, t % XR, load=t + XR < NSLOT)

            def load_neg(h, slot):
                sp.wait_ge(neg_copied, h + 1)
                sp.dma_start(q_op[slot][KR:KM, :].rearrange("s (t p) -> s t p", p=P),
                             neg_row[:, slot, :]).then_inc(neg_loaded, 16)

            def store_o(h, slot):
                sp.wait_ge(o_copied, h + 1)
                sp.dma_start(sum_dram[bass.ds(h, 1), :].rearrange("a (b n) -> (a b) n", b=NQB),
                             o_st[slot][DH:P:VW, :]).then_inc(sum_stored, 16)
                for b in range(NQB):
                    sp.dma_start(o_dram[bass.ds(h * DH, DH), QB * b:QB * b + QB],
                                 o_st[slot][VW * b:VW * b + DH, :]).then_inc(o_stored, 16)
                sp.wait_ge(sum_stored, (h + 1) * 16)
                sp.dma_start(sum_c[:, slot, :], sum_dram[bass.ds(h, 1), :].rearrange("a (p f) -> (a p) f", p=P)
                             ).then_inc(sum_in, 16)

            def store_recip(h, slot):
                sp.wait_ge(recip_done, h + 1)
                sp.dma_start(recip_dram[bass.ds(h, 1), :].rearrange("a (p f) -> (a p) f", p=P),
                             recip_c[:, slot, :]).then_inc(recip_stored, 16)

            def head_step(h, k, first=False, load=True, turn=True):
                if load:
                    if not first:
                        sp.wait_ge(scored, h * UNITS)
                    load_head(h + 2, (k + 2) % RING)
                if not first:
                    store_o(h - 1, (k - 1) % RING)
                if turn:
                    load_neg(h + 1, (k + 1) % RING)
                if not first:
                    store_recip(h - 1, (k - 1) % RING)

            def load_attn(h0, h1, done):
                m, p0, p1 = h0 * DH // P, h0 * DH % P, (h1 - 1) * DH % P + DH
                sp.wait_ge(o_stored, 16 * NQB * h1)
                sp.dma_start(attnT[p0:p1, m, :], o_dram[h0 * DH:h1 * DH, :]).then_inc(done, 16)
                sp.wait_ge(recip_stored, 16 * h1)
                for h in range(h0, h1):
                    sp.dma_start(recips[h * DH % P:h * DH % P + DH, m, :],
                                 recip_dram[h:h + 1, :].broadcast_to([DH, S])).then_inc(done, 16)

            load_neg(0, 0)
            for t in tail[-2:]:
                expert_step(t, t % XR, load=False)
            head_step(0, 0, first=True)
            head_step(1, 1)
            with sp.Fori(0, ROUNDS) as i:
                for j in range(RING):
                    head_step(i * RING + 2 + j, (2 + j) % RING)
            load_attn(0, HEADS // 2, attn_in[0])
            head_step(14, 2, load=False)
            load_attn(HEADS // 2, HEADS - 2, attn_in[1])
            head_step(15, 0, load=False, turn=False)
            load_attn(HEADS - 2, HEADS - 1, attn_in[2])
            sp.wait_ge(o_copied, HEADS)
            for b in range(NQB):
                sp.dma_start(attnT[P - DH:P, HC - 1, QB * b:QB * b + QB],
                             o_st[0][VW * b:VW * b + DH, :]).then_inc(last_in[b], 16)
            sp.wait_ge(last_inverted, 1)
            for b in range(NQB):
                sp.dma_start(recips[P - DH:P, HC - 1, QB * b:QB * b + QB],
                             last_recip[VW * b + DH:VW * b + 2 * DH, :]).then_inc(last_in[b], 16)

            ov = out_d.rearrange("(t p) d -> p t d", p=P)
            for pair in range(NT // 2):
                sp.wait_ge(out_ready, pair + 1)
                sp.dma_start(ov[:, 2 * pair:2 * pair + 2, :], x_sb[:, 2 * pair:2 * pair + 2, :]
                             ).then_inc(out_stored, 16)
            sp.wait_ge(out_stored, 16 * (NT // 2))

        @block.gpsimd
        def _(pool):
            pool.memset(zeros[:], 0.0).then_inc(zero_ready, 1)
            pool.wait_ge(zero_ready, 1)
            pool.wait_ge(x_in[3], 16)
            pool.dma_start(xs_dram.rearrange("(t p) d -> p t d", p=P),
                           zeros[:].rearrange("p (a d) -> p a d", a=1).broadcast_to([P, NSLOT, HID])
                           ).then_inc(zero_filled, 16)
            for n in range(RING):
                pool.memset(k_op[n][KR:KM, :], 1.0).then_inc(ones_ready, 1)
                pool.wait_ge(ones_ready, n + 1)
            pool.memset(v_all[:], 1.0).then_inc(ones_ready, 1)

            pool.wait_ge(zero_filled, 16)
            pool.wait_ge(route_ready, 1)
            for t in range(NT):
                pool.indirect_dma_start(
                    out=xs_dram, out_offset=bass.IndirectOffsetOnAxis(ap=row_of[:, t:t + 1], axis=0),
                    in_=xn[:, t, :], in_offset=None).then_inc(scattered, 16)

            pool.wait_ge(scattered, 16 * NT)
            for t in range(XR):
                pool.dma_start(xs[t], xs_dram[P * t:P * t + P, :]).then_inc(xs_first, 16)

            form_lowest(pool, LOW_ON_POOL[0])
            form_lowest(pool, LOW_ON_POOL[1])

            def copy_v(h, slot):
                pool.tensor_copy(v_op[slot][:], v_all[:, bass.ds(h * (NCH * VW), NCH * VW)]
                                 ).then_inc(v_loaded, 1)

            pool.wait_ge(v_read, NCH)
            for h in range(RING):
                copy_v(h, h)

            form_lowest(pool, LOW_ON_POOL[2])

            for n in range(XR):
                pool.wait_ge(ys_stored[n], 16 * len(range(n, NSLOT, XR)))
            for t in range(NT):
                pool.indirect_dma_start(
                    out=y_tok[:, t, :], out_offset=None, in_=y_dram,
                    in_offset=bass.IndirectOffsetOnAxis(ap=row_of[:, t:t + 1], axis=0)
                ).then_inc(gathered, 16)

            pool.wait_ge(wv_in, 32)
            for t in range(NT):
                ins = pool.tensor_tensor(x_sb[:, t, :], x_sb[:, t, :], bvo[:, HID:2 * HID], ALU.add)
            ins.then_inc(residual_ready, 1)

            with pool.Fori(1, 5) as i:
                for k in range(RING):
                    pool.wait_ge(pv_done, (i * RING + (k - 2)) * NCH)
                    copy_v(i * RING + k, k)
            pool.wait_ge(pv_done, (HEADS - 1 - 2) * NCH)
            copy_v(HEADS - 1, 0)

        @block.tensor
        def _(pe):
            def turn_pair(pair):
                b = pair % 4
                if pair >= 4:
                    pe.wait_ge(xnT_ready, pair - 3)
                if pair % 2 == 0 or pair == NT // 2 - 1:
                    pe.wait_ge(xn_ready, pair // 2 + 1)
                else:
                    pe.wait_ge(xn_on_act, pair // 2 + 1)
                for m in range(HC):
                    for j in range(2):
                        ins = pe.transpose(bank(b)[:, 256 * m + P * j:256 * m + P * j + P],
                                           xn[:, 2 * pair + j, P * m:P * m + P], ident)
                ins.then_inc(xT_in_psum, 1)

            def logits_block(b):
                if b == 0:
                    pe.wait_ge(rt_in, 16)
                pe.wait_ge(xnT_ready, min(2 * b + 2, NT // 2 - 1))
                if b == NQB - 1:
                    pe.wait_ge(last_xnT_ready, 1)
                for m in range(HC):
                    ins = pe.matmul(bank(4)[VW * b:VW * b + VW, :], rt[:, VW * m:VW * m + VW],
                                    xnT[:, m, QB * b:QB * b + QB], start=m == 0, stop=m == HC - 1)
                return ins

            pe.wait_ge(const_in, 16)
            for pair in range(NT // 2):
                turn_pair(pair)
                if pair == 3:
                    logits_block(0)
            for b in range(1, NQB):
                ins = logits_block(b)
            ins.then_inc(logits_T_ready, 1)
            pe.wait_ge(logits_T_copied, 1)
            for j in range(QB // P):
                ins = pe.transpose(bank(7)[:, P * j:P * j + P], logits_T[:, P * j:P * j + P], ident)
            ins.then_inc(logits_ready, 1)

            def project_v(c):
                c0, rows, tile = CHUNKS[c]
                if c == 0:
                    pe.wait_ge(wv_in, 32)
                if c == 1:
                    pe.wait_ge(rank_read, 1)
                if 2 <= c <= 4:
                    pe.wait_ge(v_read, c - 1)
                if c == 5:
                    pe.wait_ge(proj_read, 4 * 3)
                for m in range(HC):
                    ins = pe.matmul(bank(VBANKS[c])[0:rows, 0:HID], xnT[:, m, P * tile:P * tile + rows],
                                    wv[:, HID * m:HID * m + HID], start=m == 0, stop=m == HC - 1)
                ins.then_inc(v_in_psum, 1)

            pe.wait_ge(wqk_in, 32)
            for u, (is_q, t0, n, c0) in enumerate(PROJ):
                if u == RANK_AT:
                    pe.wait_ge(hot_ready, 1)
                    hot = te["hot"][:].rearrange("p t e -> p (t e)")
                    pe.matmul(bank(7)[:, 0:NT * E], tri, hot, start=True, stop=True)
                    pe.matmul(bank(7)[:, NT * E:2 * NT * E], ones, hot, start=True,
                              stop=True).then_inc(rank_ready, 1)
                if RING <= u < LAST:
                    pe.wait_ge(proj_read, 4 * (u - RING + 1))
                if u == LAST:
                    pe.wait_ge(v_read, 4)
                for odd in range(2):
                    for m in range(HC):
                        ins = pe.matmul(bank(PBANKS[u][odd])[:, 0:n],
                                        wqk[:, is_q, HID * m + P * odd:HID * m + P * odd + P],
                                        xnT[:, m, t0:t0 + n], start=m == 0, stop=m == HC - 1)
                ins.then_inc(proj_ready, 1)
                for c in V_AFTER.get(u, ()):
                    project_v(c)

            def turn_rows(t, slot, rnd):
                if isinstance(t, int) and t < XR:
                    pe.wait_ge(xs_first, 16 * XR)
                else:
                    pe.wait_ge(xs_in[slot], rnd * 16)
                if not isinstance(t, int) or t > 0:
                    pe.wait_ge(xsT_ready, t)
                for m in range(HC):
                    ins = pe.transpose(bank(2)[:, P * m:P * m + P], xs[slot][:, P * m:P * m + P], ident)
                ins.then_inc(xs_turned, 1)

            def gate_up(t, b, free=True):
                e = pe.value_load(expert[0:1, bass.ds(t, 1)], min_val=0, max_val=E - 1)
                pe.wait_ge(xsT_ready, t + 1)
                if free:
                    pe.wait_ge(hid_done, t - 1)
                for m in range(HC):
                    ins = pe.matmul(bank(b)[:, 0:2 * I], xsT[b][:, P * m:P * m + P],
                                    gu[:, bass.ds(e * (HC * 2 * I) + 2 * I * m, 2 * I)],
                                    start=m == 0, stop=m == HC - 1)
                ins.then_inc(gu_done, 1)

            def down(t, b, free=True):
                e = pe.value_load(expert[0:1, bass.ds(t, 1)], min_val=0, max_val=E - 1)
                pe.wait_ge(hidT_ready, t + 1)
                if free:
                    pe.wait_ge(ys_ready, t - 1)
                for m in range(2):
                    ins = pe.matmul(bank(4 + b)[:, 0:HID], hidT[b][:, P * m:P * m + P],
                                    dn[:, bass.ds(e * (2 * HID) + HID * m, HID)],
                                    start=m == 0, stop=m == 1)
                ins.then_inc(down_done, 1)

            def turn_hidden(t, b):
                pe.wait_ge(hid_done, t + 1)
                if not isinstance(t, int) or t > 0:
                    pe.wait_ge(hidT_ready, t)
                for m in range(2):
                    ins = pe.transpose(bank(3)[0:IH, P * m:P * m + P], hid[b][:, IH * m:IH * m + IH], ident)
                ins.then_inc(hid_turned, 1)

            def early_max_tile(t):
                pe.wait_ge(max_reduced, t)
                for c0, n in ((0, 512), (512, NK - 512)):
                    ins = pe.matmul(ps[:, EARLY_MAX + c0:EARLY_MAX + c0 + n], q_op[0][0:KR, bass.ds(t * P, P)],
                                    k_op[0][0:KR, c0:c0 + n], start=True, stop=True)
                ins.then_inc(max_scored, 1)

            def max_tile(h, t, slot, at=None):
                pe.wait_ge(max_reduced, h * NT + t - 1)
                if at is None:
                    at = 1024 * (t % 2)
                    if t == 3:
                        pe.wait_ge(neg_copied, h)
                    if t == 1:
                        turn_neg(h - 1, (slot - 1) % RING)
                for c0, n in ((0, 512), (512, NK - 512)):
                    ins = pe.matmul(ps[:, at + c0:at + c0 + n], q_op[slot][0:KR, P * t:P * t + P],
                                    k_op[slot][0:KR, c0:c0 + n], start=True, stop=True)
                ins.then_inc(max_scored, 1)

            def turn_neg(h, slot, into=turned_neg):
                pe.wait_ge(neg_ready, h + 1)
                pe.transpose(into, neg[:, slot, :], id16[:]).then_inc(neg_turned, 1)

            def expert_step(s, j, rnd):
                static = isinstance(s, int)
                if not static or s < NSLOT:
                    gate_up(s, j % 2, not static or s >= 2)
                if not static:
                    early_max_tile(s - XB)
                elif s == XE:
                    turn_neg(0, 0, early_turned_neg)
                if not static or s + 1 < NSLOT:
                    turn_rows(s + 1, (j + 1) % XR, rnd)
                if not static or s >= 2:
                    down(s - 2, j % 2, not static or s >= 4)
                if static and s == XE + 1:
                    pe.wait_ge(qk_loaded, 2 * LOADS)
                    pe.wait_ge(neg_copied, 1)
                    max_tile(1, 0, 1, FIRST_AT[0])
                if not static or 1 <= s <= NSLOT:
                    turn_hidden(s - 1, (j + 1) % 2)
                if static and s == XE + 1:
                    max_tile(1, 1, 1, FIRST_AT[1])
                if static and s == XE + 2:
                    max_tile(1, 2, 1, FIRST_AT[2])

            pe.wait_ge(proj_read, 4 * LAST)
            pe.wait_ge(v_read, NCH)
            pe.wait_ge(expert_w_in, 32)
            turn_rows(0, 0, 0)
            for s in range(XB):
                expert_step(s, s % XR, (s + 1) // XR)
            pe.wait_ge(qk_loaded, LOADS)
            pe.wait_ge(proj_read, 4 * NPROJ)
            with pe.Fori(0, XROUNDS // 2) as i:
                for j in range(XB, XB + XR):
                    expert_step(i * XR + j, j % XR, i + (j + 1) // XR)
            pe.wait_ge(late_q_loaded, 6 * 16)
            with pe.Fori(XROUNDS // 2, XROUNDS) as i:
                for j in range(XB, XB + XR):
                    expert_step(i * XR + j, j % XR, i + (j + 1) // XR)
            for s in range(XE, NSLOT + 2):
                expert_step(s, s % XR, (s + 1) // XR)

            def pv(h, c, slot, head0=False):
                rows = CHUNKS[c][1]
                pe.wait_ge(exp_done, h * UNITS + NQB * (c + 1))
                if c == 0:
                    pe.wait_ge(v_loaded, h + 1)
                    if not head0:
                        pe.wait_ge(o_copied, h)
                for b in range(NQB):
                    ins = pe.matmul(bank(7)[VW * b:VW * b + VW, :], v_op[slot][0:rows, VW * c:VW * c + VW],
                                    prob[c][0:rows, QB * b:QB * b + QB],
                                    start=c == 0, stop=c == NCH - 1)
                ins.then_inc(pv_done, 1)

            def head_step(h, k, first=False, rest_of_next=True, start_after=True):
                u = j = p = 0
                for what in ORDER:
                    if what == "S":
                        c, b = divmod(u, NQB)
                        c0, rows, _ = CHUNKS[c]
                        if not (first and u < RING):
                            pe.wait_ge(exp_done, h * UNITS + u - (RING - 1))
                        if u == 0:
                            pe.wait_ge(neg_loaded, (h + 1) * 16)
                        pe.matmul(bank(4 + u % RING)[0:rows, :], k_op[k][:, c0:c0 + rows],
                                  q_op[k][:, QB * b:QB * b + QB], start=True, stop=True).then_inc(scored, 1)
                        u += 1
                    elif what == "M":
                        if j < NT // 2 and rest_of_next:
                            max_tile(h + 1, NT // 2 + j, (k + 1) % RING)
                        if j >= NT // 2 and start_after:
                            if j == NT // 2:
                                pe.wait_ge(qk_loaded, (h + 3) * LOADS)
                            max_tile(h + 2, j - NT // 2, (k + 2) % RING)
                        if j == NT // 2 + 1 and rest_of_next and not start_after:
                            pe.wait_ge(max_reduced, (h + 2) * NT)
                            turn_neg(h + 1, (k + 1) % RING)
                        j += 1
                    else:
                        if p > 0:
                            pv(h, p - 1, k, first)
                        elif not first:
                            pv(h - 1, NCH - 1, (k - 1) % RING)
                        p += 1

            pe.wait_ge(ones_ready, RING + 1)
            pe.wait_ge(hidT_ready, NSLOT)
            pe.wait_ge(ys_ready, NSLOT)
            for t in range(3, NT // 2):
                max_tile(1, t, 1, FIRST_AT.get(t, 1024 * (t % 2)))
            head_step(0, 0, first=True)
            head_step(1, 1)
            with pe.Fori(0, ROUNDS) as i:
                for j in range(RING):
                    head_step(i * RING + 2 + j, (2 + j) % RING)
            head_step(14, 2, start_after=False)
            head_step(15, 0, rest_of_next=False, start_after=False)
            pv(15, NCH - 1, 0)

            def out_tile(t, m):
                pe.wait_ge(attn_ready, NQB * m + t // 4 + 1)
                ins = pe.matmul(ps[:, HID * t:HID * t + HID], attnT[:, m, P * t:P * t + P],
                                wo[:, HID * m:HID * m + HID], start=m == 0 and t % 2 == 0,
                                stop=m == HC - 1, skip_group_check=True)
                if m == HC - 1 and t % 2 == 1:
                    ins.then_inc(out_proj, 1)

            pe.wait_ge(wo_in, 16)
            pe.wait_ge(neg_copied, HEADS)
            for m in range(HC):
                for t in range(NT):
                    if m == 0 and t == NT // 2:
                        pe.wait_ge(exp_done, HEADS * UNITS)
                        pe.wait_ge(o_copied, HEADS)
                    out_tile(t, m)

        @block.vector
        def _(dve):
            steps = [0]

            def step(ins):
                steps[0] += 1
                ins.then_inc(dve_step, 1)

            def settle():
                dve.wait_ge(dve_step, steps[0])

            def moments(g):
                for t in range(4 * g, 4 * g + 4):
                    if t == 0:
                        dve.wait_ge(x_first, 16)
                    elif t == 2 or t % 4 == 0:
                        dve.wait_ge(x_in[g], 16)
                    step(dve.bn_stats(stats[:, t, :], x_sb[:, t, :]))
                settle()
                for t in range(4 * g, 4 * g + 4):
                    step(dve.bn_aggr(mv[:, t, :], stats[:, t, :]))
                settle()
                dve.tensor_scalar(var[:, 4 * g:4 * g + 4], mv[:, 4 * g:4 * g + 4, 1], EPS, None,
                                  ALU.add).then_inc(var_ready, 1)

            def normalize(g):
                dve.wait_ge(std_ready, g + 1)
                step(dve.reciprocal(rstd[:, 4 * g:4 * g + 4], std[:, 4 * g:4 * g + 4]))
                settle()
                dve.scalar_tensor_tensor(shift[:, 4 * g:4 * g + 4], mv[:, 4 * g:4 * g + 4, 0], -1.0,
                                         rstd[:, 4 * g:4 * g + 4], ALU.mult, ALU.mult).then_inc(scale_ready, 1)
                for t in range(4 * g, 4 * g + (2 if g < 3 else 4)):
                    ins = dve.tensor_scalar(xn[:, t, :], x_sb[:, t, :], mv[:, t, 0:1], rstd[:, t:t + 1],
                                            ALU.subtract, ALU.mult)
                ins.then_inc(xn_ready, 1)

            moments(0)
            for g in range(1, 4):
                moments(g)
                normalize(g - 1)
            normalize(3)
            dve.wait_ge(const_in, 16)
            dve.tensor_copy(id16[:], ident).then_inc(id16_ready, 1)
            for s_ in scan + tiles:
                step(dve.memset(s_[:], 0.0))
            dve.wait_ge(xT_in_psum, NT // 2)
            dve.tensor_copy(xnT[:, :, S - 2 * P:S], bank(3).rearrange("p (m n) -> p m n", m=HC)
                            ).then_inc(last_xnT_ready, 1)

            def over_tokens(ap):
                return ap.rearrange("p (a e) -> p a e", a=1).broadcast_to([P, NT, E])

            def over_experts(ap):
                return ap.rearrange("p (t a) -> p t a", a=1).broadcast_to([P, NT, E])

            rev = over_tokens(const[:, C_REV:C_REV + E])
            dve.wait_ge(logits_ready, 1)
            dve.tensor_copy(te["logit"][:].rearrange("p (b j) e -> p j b e", b=NQB),
                            bank(7).rearrange("p (j b w) -> p j b w", b=NQB, w=VW)[:, :, :, 0:E]
                            ).then_inc(logits_read, 1)
            dve.wait_ge(logits_read, 1)
            step(dve.tensor_reduce(tk["top"][:], te["logit"][:], AX.X, ALU.max))
            settle()
            step(dve.tensor_tensor(te["best"][:], te["logit"][:], over_experts(tk["top"][:]), ALU.is_equal))
            settle()
            step(dve.tensor_tensor(te["rev"][:], te["best"][:], rev, ALU.mult))
            settle()
            step(dve.tensor_reduce(tk["pick"][:], te["rev"][:], AX.X, ALU.max))
            settle()
            dve.tensor_tensor(te["hot"][:], over_experts(tk["pick"][:]), rev, ALU.is_equal
                              ).then_inc(hot_ready, 1)
            dve.wait_ge(hot_ready, 1)
            step(dve.tensor_scalar(te["gone"][:], te["hot"][:], -3.0e38, None, ALU.mult))
            settle()
            step(dve.tensor_tensor(te["rest"][:], te["logit"][:], te["gone"][:], ALU.add))
            settle()
            step(dve.tensor_reduce(tk["second"][:], te["rest"][:], AX.X, ALU.max))
            settle()
            dve.tensor_tensor(tk["gap"][:], tk["second"][:], tk["top"][:], ALU.subtract
                              ).then_inc(gap_ready, 1)

            def route():
                dve.wait_ge(rank_ready, 1)
                counts = bank(7)[:, NT * E:2 * NT * E].rearrange("p (t e) -> p e t", e=E)
                step(dve.tensor_copy(te["rank"][:].rearrange("p t e -> p (t e)"), bank(7)[:, 0:NT * E]))
                dve.tensor_copy(scan[0][:, :, NT:2 * NT], counts).then_inc(rank_read, 1)
                dve.wait_ge(rank_read, 1)
                settle()
                for n, shift in enumerate((1, 2, 4, 8)):
                    step(dve.tensor_tensor(scan[n + 1][:, :, NT:2 * NT], scan[n][:, :, NT:2 * NT],
                                           scan[n][:, :, NT - shift:2 * NT - shift], ALU.add))
                    settle()
                total = scan[4][:, :, 2 * NT - 1:2 * NT]
                step(dve.tensor_tensor(
                    more[:], total.broadcast_to([P, E, NT]),
                    const[:, C_CNT:C_CNT + NT].rearrange("p (a t) -> p a t", a=1).broadcast_to([P, E, NT]),
                    ALU.is_gt))
                settle()
                step(dve.tensor_reduce(tiles[0][:, E:2 * E], more[:], AX.X, ALU.add))
                settle()
                for n, shift in enumerate((1, 2, 4)):
                    step(dve.tensor_tensor(tiles[n + 1][:, E:2 * E], tiles[n][:, E:2 * E],
                                           tiles[n][:, E - shift:2 * E - shift], ALU.add))
                    settle()
                step(dve.tensor_scalar(first_row[:], tiles[3][:, E - 1:2 * E - 1], float(P), None, ALU.mult))
                step(dve.tensor_tensor(te["offs"][:], scan[4][:, :, NT - 1:2 * NT - 1].rearrange("p e t -> p t e"),
                                       te["rank"][:], ALU.add))
                settle()
                step(dve.tensor_tensor(te["row"][:], te["offs"][:], over_tokens(first_row[:]), ALU.add))
                settle()
                step(dve.tensor_tensor(te["mine"][:], te["row"][:], te["hot"][:], ALU.mult))
                settle()
                step(dve.tensor_reduce(tk["row"][:], te["mine"][:], AX.X, ALU.add))
                settle()
                dve.tensor_copy(row_of[:], tk["row"][:]).then_inc(route_ready, 1)
                ends = tiles[3][:, E:2 * E - 1].rearrange("p (a e) -> p a e", a=1)
                step(dve.tensor_tensor(
                    past[:], ends.broadcast_to([P, NSLOT, E - 1]),
                    const[:, C_SLOT:C_SLOT + NSLOT].rearrange("p (s a) -> p s a", a=1
                                                              ).broadcast_to([P, NSLOT, E - 1]), ALU.is_le))
                settle()
                step(dve.tensor_reduce(expert_f[:], past[:], AX.X, ALU.add))
                settle()
                step(dve.tensor_copy(expert[:], expert_f[:]))
                dve.wait_ge(ratio_ready, 1)
                step(dve.tensor_scalar(tk["denom"][:], tk["ratio"][:], 1.0, None, ALU.add))
                settle()
                step(dve.reciprocal(tk["weight"][:], tk["denom"][:]))

            def products(u, first=0, end=4):
                is_q, t0, n, c0 = PROJ[u]
                r = u % RING
                dve.wait_ge(proj_ready, u + 1)
                if u >= RING:
                    wait_lowest(dve, u - RING)
                for into, odd, fn in ((0, 0, 0), (1, 1, 1), (2, 0, 1), (3, 1, 0))[first:end]:
                    col = HC * is_q + odd
                    ins = dve.scalar_tensor_tensor(rot[:, r, into, 0:n], bank(PBANKS[u][odd])[:, 0:n],
                                                   bqk[:, col:col + 1], tab[:, fn, t0:t0 + n],
                                                   ALU.add, ALU.mult)
                    ins.then_inc(proj_read, 1)

            def turn(u):
                n, r = PROJ[u][2], u % RING
                dve.wait_ge(proj_read, 4 * (u + 1))
                dve.tensor_tensor(rot[:, r, 0, 0:n], rot[:, r, 0, 0:n], rot[:, r, 1, 0:n], ALU.subtract
                                  ).then_inc(turned_ready, 1)
                dve.tensor_tensor(rot[:, r, 2, 0:n], rot[:, r, 2, 0:n], rot[:, r, 3, 0:n], ALU.add
                                  ).then_inc(turned_ready, 1)

            def rest(u):
                n, r = PROJ[u][2], u % RING
                dve.wait_ge(turned_ready, 2 * (u + 1))
                dve.wait_ge(hi_ready, u + 1)
                dve.tensor_tensor(rot[:, r, 1:4:2, 0:n], rot[:, r, 0:4:2, 0:n], parts[:, u % 2, 0, :, 0:n],
                                  ALU.subtract).then_inc(rest_ready, 1)

            v_view = v_all[:].rearrange("p (h c w) -> p h c w", h=HEADS, c=NCH)

            def add_bv(c):
                rows = CHUNKS[c][1]
                dve.wait_ge(v_in_psum, c + 1)
                dve.tensor_tensor(v_view[0:rows, :, c, 0:DH],
                                  bank(VBANKS[c])[0:rows, 0:HID].rearrange("p (h d) -> p h d", h=HEADS),
                                  bvo[0:rows, 0:HID].rearrange("p (h d) -> p h d", h=HEADS),
                                  ALU.add).then_inc(v_read, 1)

            dve.wait_ge(wqk_in, 32)
            dve.wait_ge(tab_in, 16)
            dve.wait_ge(ones_ready, RING + 1)
            dve.wait_ge(wv_in, 32)
            for u in range(LAST + 1):
                if u == RANK_AT - 1:
                    route()
                if u < LAST:
                    products(u)
                if u > 0:
                    rest(u - 1)
                if u < LAST:
                    turn(u)
                if u > 0 and u - 1 not in LOW_ON_POOL:
                    form_lowest(dve, u - 1)
                for c in V_READ_AT.get(u, ()):
                    add_bv(c)

            def early_reduce_tile(t):
                dve.wait_ge(max_scored, t + 1)
                dve.tensor_reduce(mx[:, 0, bass.ds(t, 1)], ps[:, EARLY_MAX:EARLY_MAX + NK], AX.X, ALU.max
                                  ).then_inc(max_reduced, 1)

            def reduce_tile(h, t, slot, at=None):
                dve.wait_ge(max_scored, h * NT + t + 1)
                if at is None:
                    at = 1024 * (t % 2)
                dve.tensor_reduce(mx[:, slot, t:t + 1], ps[:, at:at + NK], AX.X, ALU.max
                                  ).then_inc(max_reduced, 1)

            def negate(h, slot):
                dve.wait_ge(max_reduced, (h + 1) * NT)
                dve.tensor_scalar(neg[:, slot, 0:NT], mx[:, slot, :], -1.0, None, ALU.mult
                                  ).then_inc(neg_hi, 1)
                dve.wait_ge(neg_hi, h + 1)
                dve.scalar_tensor_tensor(neg[:, slot, NT:2 * NT], mx[:, slot, :], -1.0,
                                         neg[:, slot, 0:NT], ALU.mult, ALU.subtract
                                         ).then_inc(neg_ready, 1)

            def copy_neg(h, slot, early=False, early0=False):
                dve.wait_ge(neg_turned, h + 1)
                if not early:
                    dve.wait_ge(neg_loaded, (h - 2) * 16)
                dve.tensor_copy(neg_row[:, slot, :], early_turned_neg if early0 else turned_neg
                                ).then_inc(neg_copied, 1)

            def expert_step(s, b):
                static = isinstance(s, int)
                if not static:
                    early_reduce_tile(s - XB)
                if not static or s < NSLOT:
                    dve.wait_ge(tanh_done, s + 1)
                    if not static or s >= 2:
                        dve.wait_ge(hid_done, s - 1)
                    dve.scalar_tensor_tensor(ga[b], th[b], 1.0, bank(b)[:, 0:I], ALU.add, ALU.mult
                                             ).then_inc(half_done, 1)
                    dve.wait_ge(half_done, s + 1)
                    if not static or s >= 2:
                        dve.wait_ge(hid_turned, s - 1)
                    dve.scalar_tensor_tensor(hid[b], ga[b], 0.5, bank(b)[:, I:2 * I], ALU.mult, ALU.mult
                                             ).then_inc(hid_done, 1)
                if not static or 1 <= s <= NSLOT:
                    dve.wait_ge(hid_turned, s)
                    if not static or s >= 3:
                        dve.wait_ge(down_done, s - 2)
                    dve.tensor_copy(hidT[1 - b], bank(3)[0:IH, 0:2 * P]).then_inc(hidT_ready, 1)

            for s in range(XB):
                expert_step(s, s % 2)
                if s < 2:
                    products(LAST, 2 * s, 2 * s + 2)
                elif s == 2:
                    turn(LAST)
                elif s == 3:
                    rest(LAST)
            with dve.Fori(0, XROUNDS) as i:
                for j in range(XB, XB + XR):
                    expert_step(i * XR + j, j % 2)
            negate(0, 0)
            for s in range(XE, NSLOT + 1):
                expert_step(s, s % 2)
                if s == XE:
                    copy_neg(0, 0, early=True, early0=True)

            def invert(h, slot):
                dve.wait_ge(sum_in, (h + 1) * 16)
                if not (isinstance(h, int) and h == 0):
                    dve.wait_ge(recip_stored, h * 16)
                dve.reciprocal(recip_c[:, slot, :], sum_c[:, slot, :]).then_inc(recip_done, 1)

            def head_step(h, k, rest_of_next=True, start_after=True, early=False):
                if rest_of_next:
                    for t in range(NT // 2, NT):
                        reduce_tile(h + 1, t, (k + 1) % RING)
                    negate(h + 1, (k + 1) % RING)
                if start_after:
                    for t in range(2):
                        reduce_tile(h + 2, t, (k + 2) % RING)
                if rest_of_next:
                    copy_neg(h + 1, (k + 1) % RING, early)
                if start_after:
                    for t in range(2, NT // 2):
                        reduce_tile(h + 2, t, (k + 2) % RING)
                if not (isinstance(h, int) and h == 0):
                    invert(h - 1, (k - 1) % RING)

            for t in range(NT // 2):
                reduce_tile(1, t, 1, FIRST_AT.get(t))
            head_step(0, 0, early=True)
            head_step(1, 1, early=True)
            with dve.Fori(0, ROUNDS) as i:
                for j in range(RING):
                    head_step(i * RING + 2 + j, (2 + j) % RING)
            head_step(14, 2, start_after=False)

            def divide(m, p0, p1, b, done=None):
                rows = slice(p0, p1)
                cols = slice(QB * b, QB * b + QB)
                ins = dve.tensor_tensor(attnT[rows, m, cols], attnT[rows, m, cols], recips[rows, m, cols],
                                        ALU.mult)
                if done is not None:
                    ins.then_inc(done, 1)

            dve.wait_ge(attn_in[0], 16 * (1 + HEADS // 2))
            for b in range(NQB):
                divide(0, 0, P, b, attn_ready)
            dve.wait_ge(residual_ready, 1)
            dve.wait_ge(gathered, 16 * NT)
            for t in range(NT):
                dve.scalar_tensor_tensor(x_sb[:, t, :], y_tok[:, t, :], tk["weight"][:, t:t + 1],
                                         x_sb[:, t, :], ALU.mult, ALU.add).then_inc(y_added, 1)
            invert(14, 2)
            dve.wait_ge(attn_in[1], 16 * (1 + HEADS // 2 - 2))
            for b in range(NQB):
                divide(1, 0, P - 2 * DH, b)
            dve.wait_ge(o_copied, HEADS)
            dve.wait_ge(o_stored, 16 * NQB * (HEADS - 2))
            dve.reciprocal(last_recip[:], o_st[0][:]).then_inc(last_inverted, 1)
            dve.wait_ge(attn_in[2], 32)
            for b in range(NQB):
                dve.wait_ge(last_in[b], 32)
                divide(1, P - 2 * DH, P, b, attn_ready)
            dve.wait_ge(y_added, NT)
            for pair in range(NT // 2):
                dve.wait_ge(out_proj, pair + 1)
                both = x_sb[:, 2 * pair:2 * pair + 2, :].rearrange("p t d -> p (t d)")
                dve.tensor_tensor(both, bank(pair), both, ALU.add).then_inc(out_ready, 1)

        @block.scalar
        def _(act):
            def root(g):
                act.wait_ge(var_ready, g + 1)
                act.activation(std[:, 4 * g:4 * g + 4], var[:, 4 * g:4 * g + 4], ACT.Sqrt
                               ).then_inc(std_ready, 1)

            def copy_xT(pair):
                act.wait_ge(xT_in_psum, pair + 1)
                act.copy(xnT[:, :, 2 * P * pair:2 * P * pair + 2 * P],
                         bank(pair % 4).rearrange("p (m n) -> p m n", m=HC)).then_inc(xnT_ready, 1)

            def normalize(g):
                act.wait_ge(scale_ready, g + 1)
                for t in range(4 * g + 2, 4 * g + 4):
                    ins = act.activation(xn[:, t, :], x_sb[:, t, :], ACT.Identity, bias=shift[:, t:t + 1],
                                         scale=rstd[:, t:t + 1])
                ins.then_inc(xn_on_act, 1)

            root(0)
            for g in range(1, 4):
                root(g)
                normalize(g - 1)
                copy_xT(2 * g - 2)
                copy_xT(2 * g - 1)
            copy_xT(6)
            act.wait_ge(logits_T_ready, 1)
            act.copy(logits_T[:], bank(4)).then_inc(logits_T_copied, 1)

            act.wait_ge(gap_ready, 1)
            act.activation(tk["ratio"][:], tk["gap"][:], ACT.Exp).then_inc(ratio_ready, 1)

            def highest(u):
                n, r = PROJ[u][2], u % RING
                act.wait_ge(turned_ready, 2 * (u + 1))
                if u >= 2:
                    act.wait_ge(parts_stored[u % 2], 48 * (u // 2))
                act.copy(parts[:, u % 2, 0, :, 0:n], rot[:, r, 0:4:2, 0:n]).then_inc(hi_ready, 1)

            def middle(u):
                n, r = PROJ[u][2], u % RING
                act.wait_ge(rest_ready, u + 1)
                act.copy(parts[:, u % 2, 1, :, 0:n], rot[:, r, 1:4:2, 0:n]).then_inc(mid_ready, 1)

            for u in range(LAST - 1):
                highest(u)
                middle(u)
            highest(LAST - 1)

            def copy_rows(t, b, static_first=False):
                act.wait_ge(xs_turned, t + 1)
                if not static_first:
                    act.wait_ge(gu_done, t - 1)
                act.copy(xsT[b], bank(2)[:, 0:HC * P]).then_inc(xsT_ready, 1)

            def expert_step(s, j, rnd):
                static = isinstance(s, int)
                b = j % 2
                if not static or s < NSLOT:
                    act.wait_ge(gu_done, s + 1)
                    if not static or s >= 2:
                        act.wait_ge(half_done, s - 1)
                    act.activation(th[b], bank(b)[:, 0:I], ACT.Tanh, scale=0.5).then_inc(tanh_done, 1)
                if not static or s + 1 < NSLOT:
                    copy_rows(s + 1, 1 - b, static and s + 1 < 2)
                if not static or s >= 2:
                    slot = (j - 2) % XR
                    act.wait_ge(down_done, s - 1)
                    if not static or rnd > 0:
                        act.wait_ge(ys_stored[slot], rnd * 16)
                    act.copy(ys[slot][:], bank(4 + b)[:, 0:HID]).then_inc(ys_ready, 1)

            copy_rows(0, 0, True)
            middle(LAST - 1)
            wait_lowest(act, 3)
            for s in range(XB):
                expert_step(s, s % XR, (s - 2) // XR)
                if s == 3:
                    highest(LAST)
                if s == 4:
                    middle(LAST)
            with act.Fori(0, XROUNDS) as i:
                for j in range(XB, XB + XR):
                    expert_step(i * XR + j, j % XR, i + (j - 2) // XR)
            for s in range(XE, NSLOT + 2):
                expert_step(s, s % XR, (s - 2) // XR)

            def copy_o(h, slot):
                act.wait_ge(pv_done, (h + 1) * NCH)
                if not (isinstance(h, int) and h == 0):
                    act.wait_ge(o_stored, h * (16 * NQB))
                act.copy(o_st[slot][:], bank(7)).then_inc(o_copied, 1)

            def head_step(h, k, first=False):
                for u in range(UNITS):
                    c, b = divmod(u, NQB)
                    rows = CHUNKS[c][1]
                    if b == 0 and not first:
                        act.wait_ge(pv_done, h * NCH + (c + 1 - NCH))
                    act.wait_ge(scored, h * UNITS + u + 1)
                    act.activation(prob[c][0:rows, QB * b:QB * b + QB], bank(4 + u % RING)[0:rows, :],
                                   ACT.Exp, scale=SCALE).then_inc(exp_done, 1)
                    if u == NQB and not first:
                        copy_o(h - 1, (k - 1) % RING)

            head_step(0, 0, first=True)
            head_step(1, 1)
            with act.Fori(0, ROUNDS) as i:
                for j in range(RING):
                    head_step(i * RING + 2 + j, (2 + j) % RING)
            for h in (14, 15):
                head_step(h, h % RING)
            copy_o(HEADS - 1, 0)


def _tables():
    import numpy as np
    f = np.float32
    theta = f(1.0) / np.power(f(10000.0), np.arange(0, DH, 2, dtype=f) / f(DH))
    angle = np.arange(S, dtype=f)[:, None] * theta[None, :]
    sin, cos = np.sin(angle).T, np.cos(angle).T
    tab = np.stack([np.tile(cos, (P // (DH // 2), 1)), np.tile(sin, (P // (DH // 2), 1))], axis=1)
    const = np.zeros((P, C_END), f)
    const[:, C_ID:C_ID + P] = np.eye(P)
    const[:, C_TRI:C_TRI + P] = np.triu(np.ones((P, P)), 1)
    const[:, C_ONE:C_ONE + P] = 1.0
    const[:, C_CNT:C_CNT + NT] = P * np.arange(NT)
    const[:, C_REV:C_REV + E] = E - np.arange(E)
    const[:, C_SLOT:C_SLOT + NSLOT] = np.arange(NSLOT)
    return np.ascontiguousarray(tab.reshape(P, 2 * S), f), const


def kernel(L0_attn_hidden_states, L0_attn_Wq, L0_attn_bq, L0_attn_Wk, L0_attn_bk, L0_attn_Wv, L0_attn_bv,
           L0_attn_Wo, L0_attn_bo, L0_ffn_router_w, L0_ffn_gate_w, L0_ffn_up_w, L0_ffn_down_w):
    import numpy as np
    import concourse.bacc as bacc
    from concourse.bass_utils import run_bass_kernel_spmd

    split = np.arange(HID).reshape(-1, 2).T.reshape(-1)

    def turned(w):
        w = np.asarray(w)
        return w.T.reshape(HC, P, -1).transpose(1, 0, 2).reshape(P, -1)

    def column(b):
        return np.asarray(b).reshape(HC, P).T

    wk, wq, bk, bq = (np.asarray(a) for a in (L0_attn_Wk, L0_attn_Wq, L0_attn_bk, L0_attn_bq))
    gate_up = np.concatenate([np.asarray(L0_ffn_gate_w), np.asarray(L0_ffn_up_w)], axis=1)
    gate_up = gate_up.transpose(0, 2, 1).reshape(E, HC, P, 2 * I).transpose(2, 0, 1, 3).reshape(P, -1)
    down = np.asarray(L0_ffn_down_w).transpose(0, 2, 1).reshape(E, 2, IH, HID).transpose(2, 0, 1, 3)
    tab, const = _tables()
    arrays = {
        "x": np.asarray(L0_attn_hidden_states).reshape(S, HID),
        "wqk": np.concatenate([turned(wk[split]), turned(wq[split])], axis=1),
        "wv": turned(L0_attn_Wv),
        "wo": turned(L0_attn_Wo),
        "bqk": np.concatenate([column(bk[split]), column(bq[split])], axis=1),
        "bvo": np.concatenate([np.asarray(L0_attn_bv), np.asarray(L0_attn_bo)]).reshape(1, 2 * HID),
        "rt": np.pad(turned(L0_ffn_router_w).reshape(P, HC, E), ((0, 0), (0, 0), (0, VW - E))).reshape(P, -1),
        "gu": gate_up,
        "dn": down.reshape(IH, -1),
        "tab": tab,
        "const": const,
    }
    arrays = {n + "_in": np.ascontiguousarray(a) for n, a in arrays.items()}
    nc = bacc.Bacc("TRN2", target_bir_lowering=False, num_devices=1)
    ins = [nc.dram_tensor(n, a.shape, F32, kind="ExternalInput").ap() for n, a in arrays.items()]
    scratch = [nc.dram_tensor(n, shape, dt, kind="Internal").ap() for n, shape, dt in (
        ("q_parts", (3, HID, S), BF16), ("k_parts", (3, HID, NK), BF16),
        ("attn_out", (HID, S), F32), ("softmax_sums", (HEADS, S), F32),
        ("softmax_recips", (HEADS, S), F32), ("sorted_rows", (NSLOT * P, HID), F32),
        ("sorted_results", (NSLOT * P, HID), F32))]
    out = nc.dram_tensor("out", (S, HID), F32, kind="ExternalOutput").ap()
    layer(nc, *ins, *scratch, out)
    res = run_bass_kernel_spmd(nc, [arrays], core_ids=[0])
    return res.results[0]["out"].reshape(1, S, HID)
```
